# Optimizing a Trainium2 kernel written in Bass

```python
import numpy as np
import jax
import jax.numpy as jnp

def _softmax(x, axis=-1):
    return jax.nn.softmax(x, axis=axis)

def _gelu(x):
    return jax.nn.gelu(x, approximate=True)

def _silu(x):
    return jax.nn.silu(x)

def _sigmoid(x):
    return jax.nn.sigmoid(x)

def _layernorm(x, axis=-1, eps=1e-05):
    m = jnp.mean(x, axis=axis, keepdims=True)
    v = jnp.var(x, axis=axis, keepdims=True)
    return (x - m) / jnp.sqrt(v + eps)

def _scatter_add(tgt, idx, src, axis=0):
    return tgt.at[idx].add(src)

def _segment_sum(src, seg, n):
    return jax.ops.segment_sum(src, seg, n)
kernel_name = 'mk_cond_resid_d2_seqx_r4_212a3d'

def setup_inputs(seed: int=0):
    np.random.seed(seed)
    _w = jnp.asarray

    def _rec_inputs():
        import jax
        import jax.numpy as jnp
        _rk = jax.random.key(seed)
        x = -1.394e-06 + 0.9999 * jax.random.normal(jax.random.fold_in(_rk, 1), (64, 64, 512), jnp.float32)
        _lenS = 64 - jax.random.randint(jax.random.fold_in(_rk, 7), (64,), 0, max(1, 64 // 4) + 1, jnp.int32)
        _lenS2 = 64 - jax.random.randint(jax.random.fold_in(_rk, 8), (64,), 0, max(1, 64 // 4) + 1, jnp.int32)
        cond_2048 = -0.00499425 + 1.0058 * jax.random.normal(jax.random.fold_in(_rk, 11), (64, 512), jnp.float32)
        return (x, cond_2048)
    x, cond_2048 = _rec_inputs()

    def _L0_cond_setup():
        import jax, jax.numpy as jnp
        import numpy as np
        B, T, D = (16, 128, 512)
        key = jax.random.key(seed)
        k0, k1, k2, k3 = jax.random.split(key, 4)
        scale = 1.0 / np.sqrt(D)
        return {'initial_state': jax.random.normal(k0, (B, D), jnp.float32), 'inputs': jax.random.normal(k1, (B, T, D), jnp.float32), 'W_ih': jax.random.normal(k2, (D, 3 * D), jnp.float32) * scale, 'W_hh': jax.random.normal(k3, (D, 3 * D), jnp.float32) * scale, 'b_ih': jnp.zeros((3 * D,), jnp.float32), 'b_hh': jnp.zeros((3 * D,), jnp.float32)}
    _L0_cond_all = _L0_cond_setup()
    _L0_cond_in = {k: v for k, v in _L0_cond_all.items() if k in ('W_ih', 'W_hh', 'b_ih', 'b_hh')}
    del _L0_cond_all

    def _L1_cond_setup():
        import jax, jax.numpy as jnp
        import numpy as np
        DT = 0.01
        EPSILON = 0.08
        ALPHA = 0.7
        BETA = 0.8
        CLAMP = 20.0
        B, T, N = (64, 128, 512)

        def _derivative(q, p, drive, coupling, bias):
            i_couple = jnp.tanh(q) @ coupling.T
            dq = q - q ** 3 / 3.0 - p + drive + i_couple + bias
            dp = EPSILON * (q + ALPHA - BETA * p)
            return (dq, dp)

        def _rk4_step(q, p, drive, coupling, bias):
            dq1, dp1 = _derivative(q, p, drive, coupling, bias)
            dq2, dp2 = _derivative(q + 0.5 * DT * dq1, p + 0.5 * DT * dp1, drive, coupling, bias)
            dq3, dp3 = _derivative(q + 0.5 * DT * dq2, p + 0.5 * DT * dp2, drive, coupling, bias)
            dq4, dp4 = _derivative(q + DT * dq3, p + DT * dp3, drive, coupling, bias)
            q_next = q + DT / 6.0 * (dq1 + 2 * dq2 + 2 * dq3 + dq4)
            p_next = p + DT / 6.0 * (dp1 + 2 * dp2 + 2 * dp3 + dp4)
            q_next = jnp.clip(q_next, -CLAMP, CLAMP)
            p_next = jnp.clip(p_next, -CLAMP, CLAMP)
            return (q_next, p_next)
        key = jax.random.key(seed)
        k1, k2, k3, k4 = jax.random.split(key, 4)
        return {'q0': jax.random.normal(k1, (B, N), dtype=jnp.float32), 'p0': jax.random.normal(k2, (B, N), dtype=jnp.float32), 'input_drive_seq': jax.random.normal(k3, (B, T, N), dtype=jnp.float32), 'coupling': jax.random.normal(k4, (N, N), dtype=jnp.float32) * 0.01, 'bias': jnp.zeros((N,), dtype=jnp.float32)}
    _L1_cond_all = _L1_cond_setup()
    _L1_cond_in = {k: v for k, v in _L1_cond_all.items() if k in ('coupling', 'bias')}
    del _L1_cond_all
    return {'x': x, 'cond_2048': cond_2048, 'L0_cond_W_ih': _L0_cond_in['W_ih'], 'L0_cond_W_hh': _L0_cond_in['W_hh'], 'L0_cond_b_ih': _L0_cond_in['b_ih'], 'L0_cond_b_hh': _L0_cond_in['b_hh'], 'L1_cond_coupling': _L1_cond_in['coupling'], 'L1_cond_bias': _L1_cond_in['bias']}

def reference(x, cond_2048, L0_cond_W_ih, L0_cond_W_hh, L0_cond_b_ih, L0_cond_b_hh, L1_cond_coupling, L1_cond_bias):
    import jax
    import jax.numpy as jnp

    def _L0_cond_ref(initial_state, inputs, W_ih, W_hh, b_ih, b_hh):
        import jax, jax.numpy as jnp
        import numpy as np
        B, T, D = (16, 128, 512)
        "ScanOverTime(GRU cell): sequential per-timestep module call with\n            dict-state passing; merge_dict_trees stacks the per-step\n            'state_predicted' tensors along axis=1 -> [B, T, D]."

        def cell(h, x):
            gi = x @ W_ih + b_ih
            gh = h @ W_hh + b_hh
            i_r, i_z, i_n = jnp.split(gi, 3, axis=-1)
            h_r, h_z, h_n = jnp.split(gh, 3, axis=-1)
            r = jax.nn.sigmoid(i_r + h_r)
            z = jax.nn.sigmoid(i_z + h_z)
            n = jnp.tanh(i_n + r * h_n)
            h_new = (1.0 - z) * n + z * h
            return (h_new, h_new)
        xs = jnp.swapaxes(inputs, 0, 1)
        _, hs = jax.lax.scan(cell, initial_state, xs)
        return jnp.swapaxes(hs, 0, 1)

    def _L1_cond_ref(q0, p0, input_drive_seq, coupling, bias):
        import jax, jax.numpy as jnp
        import numpy as np
        DT = 0.01
        EPSILON = 0.08
        ALPHA = 0.7
        BETA = 0.8
        CLAMP = 20.0
        B, T, N = (64, 128, 512)

        def _derivative(q, p, drive, coupling, bias):
            i_couple = jnp.tanh(q) @ coupling.T
            dq = q - q ** 3 / 3.0 - p + drive + i_couple + bias
            dp = EPSILON * (q + ALPHA - BETA * p)
            return (dq, dp)

        def _rk4_step(q, p, drive, coupling, bias):
            dq1, dp1 = _derivative(q, p, drive, coupling, bias)
            dq2, dp2 = _derivative(q + 0.5 * DT * dq1, p + 0.5 * DT * dp1, drive, coupling, bias)
            dq3, dp3 = _derivative(q + 0.5 * DT * dq2, p + 0.5 * DT * dp2, drive, coupling, bias)
            dq4, dp4 = _derivative(q + DT * dq3, p + DT * dp3, drive, coupling, bias)
            q_next = q + DT / 6.0 * (dq1 + 2 * dq2 + 2 * dq3 + dq4)
            p_next = p + DT / 6.0 * (dp1 + 2 * dp2 + 2 * dp3 + dp4)
            q_next = jnp.clip(q_next, -CLAMP, CLAMP)
            p_next = jnp.clip(p_next, -CLAMP, CLAMP)
            return (q_next, p_next)
        drive_tbn = jnp.swapaxes(input_drive_seq, 0, 1)

        def scan_fn(carry, drive):
            q, p = carry
            q, p = _rk4_step(q, p, drive, coupling, bias)
            return ((q, p), q)
        (_, _), q_trace_tbn = jax.lax.scan(scan_fn, (q0, p0), drive_tbn)
        return jnp.swapaxes(q_trace_tbn, 0, 1)
    x = x + _L0_cond_ref(cond_2048, x, L0_cond_W_ih, L0_cond_W_hh, L0_cond_b_ih, L0_cond_b_hh)
    x = x + _L1_cond_ref(cond_2048, cond_2048, x, L1_cond_coupling, L1_cond_bias)
    return x

_drawn_inputs = setup_inputs


def setup_inputs(seed=0):
    import zlib

    import numpy as np

    out = dict(_drawn_inputs(seed))
    spreads = {'L0_cond_b_ih': (0.0, 0.1), 'L0_cond_b_hh': (0.0, 0.1), 'L1_cond_bias': (0.0, 0.273)}
    factors = {}
    for name, (base, spread) in spreads.items():
        noise = np.random.default_rng([zlib.crc32(name.encode()), seed]).standard_normal(out[name].shape)
        drawn = base * np.exp(spread * noise) if base else spread * noise
        out[name] = jnp.asarray(drawn.astype(out[name].dtype))
    for name, factor in factors.items():
        out[name] = (out[name] * factor).astype(out[name].dtype)
    return out
```

```python
from contextlib import ExitStack

import concourse.bass as bass
from concourse import mybir

P = 128
F32 = mybir.dt.float32
F32R = mybir.dt.float32r
F16 = mybir.dt.float16
I32 = mybir.dt.int32
ALU = mybir.AluOpType
ACT = mybir.ActivationFunctionType
AX = mybir.AxisListType
RED_MAX = bass.bass_isa.ReduceOp.max

DT = 0.01
EPSILON = 0.08
ALPHA = 0.7
BETA = 0.8
CLAMP = 20.0

HALF = DT / 2
DRIFT = HALF * EPSILON
STAGE_DT = (HALF, HALF, DT, DT / 6)
B_DT = (DRIFT * BETA, DRIFT * BETA, 2 * DRIFT * BETA)
B_MAX = BETA * CLAMP - ALPHA
B_MIN = -BETA * CLAMP - ALPHA

UNROLL = 8
TAIL = 16
CHUNK = 4
SLOTS = 4
PIECES = 3
AHEAD = 9
TANH_SCALE = 2.0 ** 15


def gru_rk4_kernel(nc, x_in, cond_in, wih_in, whh_in, cpl_in, bih_in, bhh_in, bias_in, out):
    T, _, _ = x_in.shape
    K = 4
    B = 64
    KB = K * B
    M3 = 12
    assert T % UNROLL == 0 and T >= TAIL + 2 * UNROLL and UNROLL % (2 * CHUNK) == 0
    assert M3 == CHUNK * PIECES
    LAST_PIECE = T // CHUNK * M3
    FIRST_PIECES = M3 + PIECES

    ctx = ExitStack()
    with ctx:
        def sb(name, shape, dt=F32):
            return ctx.enter_context(nc.sbuf_tensor(name, shape, dt))

        def bank(name):
            return ctx.enter_context(nc.psum_tensor(name, [P, 512], F32))

        def sem(name):
            return ctx.enter_context(nc.semaphore(name))

        wih_hi = sb("wih_hi", [P, K, 1536], F32R)
        wih_lo = sb("wih_lo", [P, K, 1536], F32R)
        whh_hi = sb("whh_hi", [P, K, 1536], F16)
        whh_lo = sb("whh_lo", [P, K, 1536], F16)
        cpl_hi = sb("cpl_hi", [P, K, 512], F16)
        cpl_lo = sb("cpl_lo", [P, K, 512], F16)
        whh_raw = sb("whh_raw", [P, K * 1536])
        cpl_raw = sb("cpl_raw", [P, K * 512])
        gi = [sb(f"gi{i}", [P, M3, CHUNK, B]) for i in range(2)]
        ring = sb("ring", [P, SLOTS, KB])
        xs_raw = sb("xs_raw", [P, SLOTS, KB])
        xs_hi = [sb(f"xs_hi{i}", [P, CHUNK, K, B], F32R) for i in range(2)]
        xs_lo = [sb(f"xs_lo{i}", [P, CHUNK, K, B], F32R) for i in range(2)]

        bih = sb("bih", [P, M3])
        bhh = sb("bhh", [P, M3])
        gi_bias = sb("gi_bias", [P, M3])
        rk_bias = sb("rk_bias", [P, K])
        mags = sb("mags", [P, 3])
        allmags = sb("allmags", [P, 3])
        pow2 = sb("pow2", [P, 3])
        scale = sb("scale", [P, 3])
        gh_unscale = sb("gh_unscale", [P, 1])
        rk_unscale = sb("rk_unscale", [P, 4])

        q = sb("q", [P, 4, KB])
        q_raw = sb("q_raw", [P, KB])
        th = sb("th", [P, KB])
        th_hi = sb("th_hi", [P, KB], F16)
        th_lo = sb("th_lo", [P, KB], F16)
        sq = sb("sq", [P, KB])
        cube = sb("cube", [P, KB])
        b_state = sb("b_state", [P, KB])
        b_raw = sb("b_raw", [P, KB])
        b_mid = sb("b_mid", [P, KB])
        y = sb("y", [P, 4, KB])
        y_sum = sb("y_sum", [P, KB])
        drive = sb("drive", [P, KB])
        e0 = sb("e0", [P, KB])
        lin = sb("lin", [P, 3, KB])
        lin_full = sb("lin_full", [P, KB])
        lin_end = sb("lin_end", [P, KB])
        base = sb("base", [P, 4, KB])
        q_sum = sb("q_sum", [P, KB])

        h = sb("h", [P, KB])
        h_hi = sb("h_hi", [P, KB], F16)
        h_lo = sb("h_lo", [P, KB], F16)
        rz_in = sb("rz_in", [P, 2 * KB])
        rz = sb("rz", [P, 2 * KB])
        n_h = sb("n_h", [P, KB])
        n_rh = sb("n_rh", [P, KB])
        n_in = sb("n_in", [P, KB])
        n_gate = sb("n_gate", [P, KB])
        h_minus_n = sb("h_minus_n", [P, KB])
        z_part = sb("z_part", [P, KB])

        ps_rk = bank("ps_rk")
        ps_rz = bank("ps_rz")
        ps_n = bank("ps_n")
        ps_gi = [bank(f"ps_gi{i}") for i in range(PIECES)]

        wih_loaded = [sem(f"wih_loaded{k}") for k in range(K)]
        whh_loaded = sem("whh_loaded")
        cpl_loaded = sem("cpl_loaded")
        cond_loaded = sem("cond_loaded")
        bias_loaded = sem("bias_loaded")
        x_loaded = [sem(f"x_loaded{i}") for i in range(SLOTS)]
        xs_loaded = [sem(f"xs_loaded{i}") for i in range(SLOTS)]
        stored = [sem(f"stored{i}") for i in range(SLOTS)]
        wih_hi_ready = sem("wih_hi_ready")
        wih_lo_ready = sem("wih_lo_ready")
        mags_ready = sem("mags_ready")
        allmags_ready = sem("allmags_ready")
        prep = sem("prep")
        whh_ready = sem("whh_ready")
        cpl_ready = sem("cpl_ready")
        gi_bias_ready = sem("gi_bias_ready")
        xs_hi_ready = sem("xs_hi_ready")
        xs_lo_ready = sem("xs_lo_ready")
        gi_summed = sem("gi_summed")
        gi_ready = sem("gi_ready")
        rz_summed = sem("rz_summed")
        n_summed = sem("n_summed")
        rz_in_ready = sem("rz_in_ready")
        rz_ready = sem("rz_ready")
        n_h_ready = sem("n_h_ready")
        n_rh_ready = sem("n_rh_ready")
        n_in_ready = sem("n_in_ready")
        n_gate_ready = sem("n_gate_ready")
        h_minus_n_ready = sem("h_minus_n_ready")
        z_part_ready = sem("z_part_ready")
        h_ready = sem("h_ready")
        h_hi_ready = sem("h_hi_ready")
        h_lo_ready = sem("h_lo_ready")
        x1_ready = sem("x1_ready")
        drive_ready = sem("drive_ready")
        rk_summed = sem("rk_summed")
        q_ready = sem("q_ready")
        q_raw_ready = sem("q_raw_ready")
        th_ready = sem("th_ready")
        th_hi_ready = sem("th_hi_ready")
        th_lo_ready = sem("th_lo_ready")
        sq_ready = sem("sq_ready")
        cube_ready = sem("cube_ready")
        y_ready = sem("y_ready")
        b_mid_ready = sem("b_mid_ready")
        b_raw_ready = sem("b_raw_ready")
        b_ready = sem("b_ready")
        e0_ready = sem("e0_ready")
        lin_ready = sem("lin_ready")
        lin_full_ready = sem("lin_full_ready")
        lin_end0_ready = sem("lin_end0_ready")
        lin_end_ready = sem("lin_end_ready")
        base_ready = sem("base_ready")
        base3_ready = sem("base3_ready")
        y12_ready = sem("y12_ready")
        y_part_ready = sem("y_part_ready")
        y_sum_ready = sem("y_sum_ready")
        q_part_ready = sem("q_part_ready")
        q_sum1_ready = sem("q_sum1_ready")
        q_sum_ready = sem("q_sum_ready")
        out_ready = sem("out_ready")

        def wait(eng, s, value):
            if not isinstance(value, int) or value > 0:
                eng.wait_ge(s, value)

        def over_steps(eng, step):
            for j in range(UNROLL):
                step(0, j)
            with eng.Fori(UNROLL, T - TAIL - UNROLL + 1, UNROLL) as t0:
                for j in range(UNROLL):
                    step(t0, j)
            for j in range(TAIL):
                step(T - TAIL, j)

        def before(t0, j, limit):
            return not isinstance(t0, int) or t0 + j < limit

        def rounds(t0, j):
            return t0 * (16 // SLOTS) + 16 * (j // SLOTS + 1)

        def x_at(dram, t0, j):
            if isinstance(t0, int):
                return dram[t0 + j, :, :]
            return dram[bass.ds(t0 + j, 1), :, :].rearrange("t p n -> p (t n)")

        def splits_x(t0, j):
            return before(t0, j + AHEAD, T)

        block = ctx.enter_context(nc.Block())

        @block.sync
        def _(sp):
            sp.dma_start(bih[:, :], bih_in).then_inc(bias_loaded, 16)
            sp.dma_start(bhh[:, :], bhh_in).then_inc(bias_loaded, 16)
            sp.dma_start(rk_bias[:, :], bias_in).then_inc(bias_loaded, 16)
            for u in range(SLOTS):
                sp.dma_start(ring[:, u, :], x_at(x_in, 0, u)).then_inc(x_loaded[u], 16)
            for k in range(K):
                raw = gi[k // 2][:, :, :, :].rearrange("p m j b -> p (m j b)")
                sp.dma_start(raw[:, k % 2 * 1536:(k % 2 + 1) * 1536], wih_in[:, k, :]).then_inc(wih_loaded[k], 16)
            for u in range(SLOTS, 2 * SLOTS):
                sp.dma_start(xs_raw[:, u % SLOTS, :], x_at(x_in, 0, u)).then_inc(xs_loaded[u % SLOTS], 16)
            sp.dma_start(q[:, 0, :], cond_in).then_inc(cond_loaded, 16)
            sp.dma_start(h[:, :], cond_in).then_inc(cond_loaded, 16)
            sp.dma_start(whh_raw[:, :], whh_in).then_inc(whh_loaded, 16)
            sp.dma_start(cpl_raw[:, :], cpl_in).then_inc(cpl_loaded, 16)

            def refill_xs(t0, u):
                sp.wait_ge(xs_lo_ready, t0 + (u - SLOTS + 1))
                sp.dma_start(xs_raw[:, u % SLOTS, :], x_at(x_in, t0, u)).then_inc(xs_loaded[u % SLOTS], 16)

            for u in range(2 * SLOTS, AHEAD + SLOTS):
                refill_xs(0, u)

            def step(t0, j):
                if before(t0, j + AHEAD + SLOTS, T):
                    refill_xs(t0, j + AHEAD + SLOTS)
                if (not isinstance(t0, int) or t0 + j >= 1) and before(t0, j - 1 + SLOTS, T):
                    slot = (j - 1) % SLOTS
                    sp.wait_ge(stored[slot], rounds(t0, j - 1))
                    sp.dma_start(ring[:, slot, :], x_at(x_in, t0, j - 1 + SLOTS)).then_inc(x_loaded[slot], 16)
                sp.wait_ge(out_ready, t0 + (j + 1))
                sp.dma_start(x_at(out, t0, j), ring[:, j % SLOTS, :]).then_inc(stored[j % SLOTS], 16)
            over_steps(sp, step)
            for s in stored:
                sp.wait_ge(s, 16 * (T // SLOTS))

        @block.tensor
        def _(pe):
            def product(ps, cols, w_hi, w_lo, w_cols, v_hi, v_lo, done, lo_ready=None, lo_value=0):
                for m in range(cols):
                    dst = ps[:, m * B:(m + 1) * B]
                    for k in range(K):
                        nc.tensor.matmul(dst, w_lo[:, k, w_cols + m * P:w_cols + (m + 1) * P], v_hi[:, k * B:(k + 1) * B],
                                         start=(m == 0 and k == 0), stop=False, skip_group_check=True)
                if lo_ready is not None:
                    wait(pe, lo_ready, lo_value)
                for m in range(cols):
                    dst = ps[:, m * B:(m + 1) * B]
                    for k in range(K):
                        w = w_hi[:, k, w_cols + m * P:w_cols + (m + 1) * P]
                        nc.tensor.matmul(dst, w, v_hi[:, k * B:(k + 1) * B], start=False, stop=False, skip_group_check=True)
                        last = nc.tensor.matmul(dst, w, v_lo[:, k * B:(k + 1) * B], start=False,
                                                stop=(m == cols - 1 and k == K - 1), skip_group_check=True)
                last.then_inc(done, 1)

            def coupling(t0, j, s):
                pe.wait_ge(th_hi_ready, t0 * 4 + (4 * j + s + 1))
                product(ps_rk, K, cpl_hi, cpl_lo, 0, th_hi, th_lo, rk_summed, th_lo_ready, t0 * 4 + (4 * j + s + 1))

            def gates_rz(t0, j):
                pe.wait_ge(h_lo_ready, t0 + (j + 1))
                product(ps_rz, 2 * K, whh_hi, whh_lo, 0, h_hi, h_lo, rz_summed)

            def gates_n(t0, j):
                pe.wait_ge(h_lo_ready, t0 + (j + 1))
                product(ps_n, K, whh_hi, whh_lo, 8 * P, h_hi, h_lo, n_summed)

            def project(t0, first, offset, lo, hi):
                for n in range(lo, hi):
                    i, r = divmod(n, 3 * K)
                    k, part = divmod(r, 3)
                    g = first + i
                    m = g % M3
                    par = g // M3 % 2
                    if r == 0:
                        wait(pe, gi_ready, t0 * 3 + (g - PIECES + 1))
                    if part == 2:
                        w, v = wih_lo, xs_hi[par]
                    else:
                        w, v = wih_hi, (xs_hi, xs_lo)[part][par]
                    last = nc.tensor.matmul(ps_gi[i][:, 0:CHUNK * B].rearrange("p (j b) -> p j b", j=CHUNK),
                                            w[:, k, m * P:(m + 1) * P], v[:, :, k, :],
                                            start=(r == 0), stop=(r == 3 * K - 1))
                    if r == 3 * K - 1:
                        last.then_inc(gi_summed, 1)

            pe.wait_ge(wih_hi_ready, K)
            pe.wait_ge(wih_lo_ready, K)
            for c in range(FIRST_PIECES // PIECES):
                pe.wait_ge(xs_hi_ready, CHUNK * (1 + c * PIECES // M3))
                pe.wait_ge(xs_lo_ready, CHUNK * (1 + c * PIECES // M3))
                project(0, c * PIECES, 0, 0, PIECES * 3 * K)
            pe.wait_ge(whh_ready, 2)
            gates_rz(0, 0)
            gates_n(0, 0)
            pe.wait_ge(cpl_ready, 2)

            def step(t0, j):
                more_cells = before(t0, j + 1, T)
                first = FIRST_PIECES + 3 * j
                more_pieces = not isinstance(t0, int) or t0 * 3 + first < LAST_PIECE
                coupling(t0, j, 0)
                if more_cells:
                    gates_rz(t0, j + 1)
                coupling(t0, j, 1)
                if more_cells:
                    gates_n(t0, j + 1)
                if more_pieces:
                    pe.wait_ge(xs_hi_ready, t0 + CHUNK * (first // M3 + 1))
                    pe.wait_ge(xs_lo_ready, t0 + CHUNK * (first // M3 + 1))
                    project(t0, first, j, 0, 4)
                coupling(t0, j, 2)
                if more_pieces:
                    project(t0, first, j, 4, 20)
                coupling(t0, j, 3)
                if more_pieces:
                    project(t0, first, j, 20, 36)
            over_steps(pe, step)

        @block.scalar
        def _(act):
            def split_x_hi(t0, u):
                if isinstance(t0, int) and t0 + u < SLOTS:
                    act.wait_ge(x_loaded[u], 16)
                    src = ring
                else:
                    act.wait_ge(xs_loaded[u % SLOTS], rounds(t0, u - SLOTS))
                    src = xs_raw
                nc.scalar.activation(xs_hi[u // CHUNK % 2][:, u % CHUNK, :, :].rearrange("p k b -> p (k b)"),
                                     src[:, u % SLOTS, :], ACT.Copy).then_inc(xs_hi_ready, 1)

            def store_gi(t0, g):
                act.wait_ge(gi_summed, t0 * 3 + (g + 1))
                m = g % M3
                nc.scalar.activation(gi[g // M3 % 2][:, m, :, :].rearrange("p j b -> p (j b)"),
                                     ps_gi[g % PIECES][:, 0:CHUNK * B], ACT.Identity,
                                     bias=gi_bias[:, m:m + 1], scale=1.0).then_inc(gi_ready, 1)

            def gate_rz(t0, j):
                act.wait_ge(rz_in_ready, t0 + (j + 1))
                nc.scalar.activation(rz[:, :], rz_in[:, :], ACT.Tanh, scale=0.5).then_inc(rz_ready, 1)

            def gate_n(t0, j):
                act.wait_ge(n_in_ready, t0 + (j + 1))
                nc.scalar.activation(n_gate[:, :], n_in[:, :], ACT.Tanh).then_inc(n_gate_ready, 1)

            def nonlinear(t0, j, s):
                wait(act, q_ready, t0 * 4 + (4 * j + s))
                wait(act, th_lo_ready, t0 * 4 + (4 * j + s))
                nc.scalar.activation(th[:, :], q[:, s, :], ACT.Tanh).then_inc(th_ready, 1)
                wait(act, cube_ready, t0 * 4 + (4 * j + s))
                nc.scalar.activation(sq[:, :], q[:, s, :], ACT.Square,
                                     scale=(STAGE_DT[s] / 3) ** 0.5).then_inc(sq_ready, 1)

            for u in range(CHUNK):
                split_x_hi(0, u)
            for k in range(K):
                act.wait_ge(wih_loaded[k], 16)
                raw = gi[k // 2][:, :, :, :].rearrange("p m j b -> p (m j b)")
                nc.scalar.activation(wih_hi[:, k, :], raw[:, k % 2 * 1536:(k % 2 + 1) * 1536],
                                     ACT.Copy).then_inc(wih_hi_ready, 1)
            for u in range(CHUNK, 2 * CHUNK):
                split_x_hi(0, u)
            act.wait_ge(gi_bias_ready, 2)
            act.wait_ge(wih_lo_ready, K)
            for g in range(FIRST_PIECES):
                store_gi(0, g)
            for u in range(2 * CHUNK, AHEAD):
                split_x_hi(0, u)
            act.wait_ge(cond_loaded, 32)
            gate_rz(0, 0)
            gate_n(0, 0)

            def step(t0, j):
                more_cells = before(t0, j + 1, T)
                first = FIRST_PIECES + 3 * j
                more_pieces = not isinstance(t0, int) or t0 * 3 + first < LAST_PIECE
                late = (not isinstance(t0, int) or t0 + j >= 1) and (not isinstance(t0, int) or t0 * 3 + first - PIECES < LAST_PIECE)
                nonlinear(t0, j, 0)
                if late:
                    store_gi(t0, first - 2)
                    store_gi(t0, first - 1)
                if splits_x(t0, j):
                    split_x_hi(t0, j + AHEAD)
                nonlinear(t0, j, 1)
                if more_cells:
                    gate_rz(t0, j + 1)
                nonlinear(t0, j, 2)
                if more_cells:
                    gate_n(t0, j + 1)
                nonlinear(t0, j, 3)
                if more_pieces:
                    store_gi(t0, first)
            over_steps(act, step)

        @block.vector
        def _(dve):
            def fma(dst, a, c, b, done, op1=ALU.add):
                nc.vector.scalar_tensor_tensor(out=dst, in0=a, scalar=c, in1=b, op0=ALU.mult, op1=op1).then_inc(done, 1)

            def split_h():
                nc.vector.tensor_scalar(h_hi[:, :], h[:, :], scale[:, 2:3], None, op0=ALU.mult).then_inc(h_hi_ready, 1)

            def cell_rz(t0, u):
                dve.wait_ge(rz_summed, t0 + (u + 1))
                dve.wait_ge(gi_ready, t0 * 3 + M3 * (u // CHUNK + 1))
                blocks = gi[u // CHUNK % 2][:, 0:8, u % CHUNK, :]
                fma(rz_in[:, :].rearrange("p (m b) -> p m b", b=B), ps_rz[:, :].rearrange("p (m b) -> p m b", b=B),
                    gh_unscale[:, 0:1], blocks, rz_in_ready)

            def cell_n_h(t0, u):
                dve.wait_ge(n_summed, t0 + (u + 1))
                fma(n_h[:, :].rearrange("p (m b) -> p m b", b=B), ps_n[:, 0:KB].rearrange("p (m b) -> p m b", b=B),
                    gh_unscale[:, 0:1], bhh[:, 8:12].unsqueeze(2).broadcast_to([P, K, B]), n_h_ready)

            def cell_n_rh(t0, u):
                dve.wait_ge(rz_ready, t0 + (u + 1))
                dve.wait_ge(n_h_ready, t0 + (u + 1))
                nc.vector.scalar_tensor_tensor(out=n_rh[:, :], in0=rz[:, 0:KB], scalar=1.0, in1=n_h[:, :],
                                               op0=ALU.add, op1=ALU.mult).then_inc(n_rh_ready, 1)

            def cell_n_in(t0, u):
                dve.wait_ge(n_rh_ready, t0 + (u + 1))
                fma(n_in[:, :].rearrange("p (m b) -> p m b", b=B), n_rh[:, :].rearrange("p (m b) -> p m b", b=B),
                    0.5, gi[u // CHUNK % 2][:, 8:12, u % CHUNK, :], n_in_ready)

            def cell_z(t0, u):
                dve.wait_ge(h_minus_n_ready, t0 + (u + 1))
                nc.vector.scalar_tensor_tensor(out=z_part[:, :], in0=rz[:, KB:2 * KB], scalar=1.0, in1=h_minus_n[:, :],
                                               op0=ALU.add, op1=ALU.mult).then_inc(z_part_ready, 1)

            def cell_h(t0, u):
                dve.wait_ge(z_part_ready, t0 + (u + 1))
                wait(dve, x1_ready, t0 + u)
                fma(h[:, :], z_part[:, :], 0.5, n_gate[:, :], h_ready)

            def split_h_hi(t0, u):
                dve.wait_ge(h_ready, t0 + (u + 1))
                split_h()

            def split_h_lo(t0, u):
                dve.wait_ge(h_hi_ready, t0 + (u + 2))
                fma(h_lo[:, :], h[:, :], scale[:, 2:3], h_hi[:, :], h_lo_ready, ALU.subtract)

            for k in range(K):
                dve.wait_ge(wih_hi_ready, k + 1)
                raw = gi[k // 2][:, :, :, :].rearrange("p m j b -> p (m j b)")
                nc.vector.tensor_tensor(wih_lo[:, k, :], raw[:, k % 2 * 1536:(k % 2 + 1) * 1536],
                                        wih_hi[:, k, :].bitcast(F32), ALU.subtract).then_inc(wih_lo_ready, 1)
            dve.wait_ge(bias_loaded, 48)
            nc.vector.tensor_tensor(gi_bias[:, 0:8], bih[:, 0:8], bhh[:, 0:8], ALU.add).then_inc(gi_bias_ready, 1)
            nc.vector.tensor_copy(gi_bias[:, 8:12], bih[:, 8:12]).then_inc(gi_bias_ready, 1)
            nc.vector.tensor_scalar(rk_bias[:, :], rk_bias[:, :], -ALPHA / BETA, None, op0=ALU.add).then_inc(prep, 1)
            dve.wait_ge(cond_loaded, 32)
            nc.vector.tensor_scalar(b_state[:, :], q[:, 0, :], BETA, -ALPHA, op0=ALU.mult, op1=ALU.add).then_inc(prep, 1)
            nc.vector.tensor_reduce(mags[:, 2:3], q[:, 0, :], AX.X, ALU.max, apply_absolute_value=True).then_inc(prep, 1)
            dve.wait_ge(whh_loaded, 16)
            nc.vector.tensor_reduce(mags[:, 0:1], whh_raw[:, :], AX.X, ALU.max, apply_absolute_value=True).then_inc(prep, 1)
            dve.wait_ge(cpl_loaded, 16)
            nc.vector.tensor_reduce(mags[:, 1:2], cpl_raw[:, :], AX.X, ALU.max, apply_absolute_value=True).then_inc(mags_ready, 1)
            dve.wait_ge(allmags_ready, 1)
            dve.wait_ge(mags_ready, 1)
            nc.vector.tensor_scalar(mags[:, 0:2], allmags[:, 0:2], 2.0 ** -100, None, op0=ALU.max).then_inc(prep, 1)
            nc.vector.tensor_scalar(mags[:, 2:3], allmags[:, 2:3], 1.0, None, op0=ALU.max).then_inc(prep, 1)
            dve.wait_ge(prep, 6)
            nc.vector.tensor_scalar(pow2[:, :].bitcast(I32), mags[:, :].bitcast(I32), 0x7F800000, None,
                                    op0=ALU.bitwise_and).then_inc(prep, 1)
            dve.wait_ge(prep, 7)
            nc.vector.tensor_scalar(pow2[:, :], pow2[:, :], 2.0 ** -14, None, op0=ALU.mult).then_inc(prep, 1)
            dve.wait_ge(prep, 8)
            nc.vector.reciprocal(scale[:, :], pow2[:, :]).then_inc(prep, 1)
            nc.vector.tensor_tensor(gh_unscale[:, :], pow2[:, 0:1], pow2[:, 2:3], ALU.mult).then_inc(prep, 1)
            for s in range(4):
                nc.vector.tensor_scalar(rk_unscale[:, s:s + 1], pow2[:, 1:2], STAGE_DT[s] / TANH_SCALE, None,
                                        op0=ALU.mult).then_inc(prep, 1)
            dve.wait_ge(prep, 14)
            split_h()
            flat = [w[:, :, :].rearrange("p k n -> p (k n)") for w in (whh_hi, whh_lo, cpl_hi, cpl_lo)]
            nc.vector.tensor_scalar(flat[0], whh_raw[:, :], scale[:, 0:1], None, op0=ALU.mult).then_inc(whh_ready, 1)
            split_h_lo(0, -1)
            dve.wait_ge(whh_ready, 1)
            fma(flat[1], whh_raw[:, :], scale[:, 0:1], flat[0], whh_ready, ALU.subtract)
            nc.vector.tensor_scalar(flat[2], cpl_raw[:, :], scale[:, 1:2], None, op0=ALU.mult).then_inc(cpl_ready, 1)
            dve.wait_ge(cpl_ready, 1)
            fma(flat[3], cpl_raw[:, :], scale[:, 1:2], flat[2], cpl_ready, ALU.subtract)

            def stage_cube(t0, j, s):
                dve.wait_ge(sq_ready, t0 * 4 + (4 * j + s + 1))
                wait(dve, q_ready, t0 * 4 + (4 * j + s))
                if s == 0:
                    wait(dve, base3_ready, t0 + j)
                else:
                    wait(dve, base_ready, t0 * 3 + (3 * j + s))
                nc.vector.scalar_tensor_tensor(out=cube[:, :], in0=sq[:, :], scalar=-STAGE_DT[s], in1=q[:, s, :],
                                               op0=ALU.add, op1=ALU.mult).then_inc(cube_ready, 1)

            def split_tanh_hi(t0, j, s):
                dve.wait_ge(th_ready, t0 * 4 + (4 * j + s + 1))
                nc.vector.tensor_scalar(th_hi[:, :], th[:, :], TANH_SCALE, None, op0=ALU.mult).then_inc(th_hi_ready, 1)

            def split_tanh_lo(t0, j, s):
                dve.wait_ge(th_hi_ready, t0 * 4 + (4 * j + s + 1))
                fma(th_lo[:, :], th[:, :], TANH_SCALE, th_hi[:, :], th_lo_ready, ALU.subtract)

            def stage_q(t0, j, s):
                dve.wait_ge(rk_summed, t0 * 4 + (4 * j + s + 1))
                if s < 3:
                    dve.wait_ge(base_ready, t0 * 3 + (3 * j + s + 1))
                    fma(q[:, s + 1, :], ps_rk[:, 0:KB], rk_unscale[:, s:s + 1], base[:, s, :], q_ready)
                else:
                    dve.wait_ge(base3_ready, t0 + (j + 1))
                    fma(q_raw[:, :], ps_rk[:, 0:KB], rk_unscale[:, s:s + 1], base[:, s, :], q_raw_ready)
                    dve.wait_ge(q_raw_ready, t0 + (j + 1))
                    nc.vector.tensor_scalar(q[:, 0, :], q_raw[:, :], -CLAMP, CLAMP, op0=ALU.max, op1=ALU.min).then_inc(q_ready, 1)

            def start_e(t0, j):
                dve.wait_ge(drive_ready, t0 + (j + 1))
                wait(dve, b_ready, t0 + j)
                fma(e0[:, :], b_state[:, :], -1.0 / BETA, drive[:, :], e0_ready)

            def start_lin(t0, j):
                dve.wait_ge(e0_ready, t0 + (j + 1))
                wait(dve, q_ready, t0 * 4 + 4 * j)
                wait(dve, base_ready, t0 * 3 + 3 * j)
                fma(lin[:, 0, :], e0[:, :], HALF, q[:, 0, :], lin_ready)
                fma(lin_full[:, :], e0[:, :], DT, q[:, 0, :], lin_full_ready)
                fma(lin_end[:, :], e0[:, :], HALF, q[:, 0, :], lin_end0_ready, ALU.subtract)

            def stage_b(t0, j, s):
                dve.wait_ge(y_ready, t0 * 4 + (4 * j + s + 1))
                fma(b_mid[:, :], y[:, s, :], B_DT[s], b_state[:, :], b_mid_ready)

            def stage_lin(t0, j, s):
                dve.wait_ge(y_ready, t0 * 4 + (4 * j + s))
                if s == 1:
                    dve.wait_ge(lin_ready, t0 * 3 + (3 * j + 1))
                    fma(lin[:, 1, :], y[:, 0, :], -HALF * DRIFT, lin[:, 0, :], lin_ready)
                else:
                    dve.wait_ge(lin_full_ready, t0 + (j + 1))
                    fma(lin[:, 2, :], y[:, 1, :], -DT * DRIFT, lin_full[:, :], lin_ready)

            def end_lin(t0, j):
                dve.wait_ge(y_ready, t0 * 4 + (4 * j + 3))
                dve.wait_ge(lin_end0_ready, t0 + (j + 1))
                fma(lin_end[:, :], y[:, 2, :], -DT * DRIFT, lin_end[:, :], lin_end_ready)

            def end_q_part(t0, j):
                dve.wait_ge(q_ready, t0 * 4 + (4 * j + 2))
                fma(q_sum[:, :], q[:, 2, :], 2.0, q[:, 1, :], q_part_ready)

            def end_y(t0, j):
                dve.wait_ge(y12_ready, t0 + (j + 1))
                fma(y_sum[:, :], y_sum[:, :], 2.0, y[:, 0, :], y_part_ready)

            def end_base(t0, j):
                dve.wait_ge(q_sum_ready, t0 + (j + 1))
                dve.wait_ge(cube_ready, t0 * 4 + (4 * j + 4))
                fma(base[:, 3, :], q_sum[:, :], 1.0 / 3, cube[:, :], base3_ready, ALU.subtract)

            def end_b(t0, j):
                dve.wait_ge(y_sum_ready, t0 + (j + 1))
                fma(b_raw[:, :], y_sum[:, :], DRIFT * BETA / 3, b_state[:, :], b_raw_ready)

            def end_b_clip(t0, j):
                dve.wait_ge(b_raw_ready, t0 + (j + 1))
                nc.vector.tensor_scalar(b_state[:, :], b_raw[:, :], B_MIN, B_MAX, op0=ALU.max, op1=ALU.min).then_inc(b_ready, 1)

            cell_rz(0, 0)
            cell_n_h(0, 0)
            cell_n_rh(0, 0)
            cell_n_in(0, 0)
            split_tanh_hi(0, 0, 0)
            split_tanh_lo(0, 0, 0)
            cell_z(0, 0)
            cell_h(0, 0)
            split_h_hi(0, 0)
            split_h_lo(0, 0)

            def step(t0, j):
                more_cells = before(t0, j + 1, T)
                more_steps = more_cells
                start_e(t0, j)
                stage_cube(t0, j, 0)
                start_lin(t0, j)
                stage_b(t0, j, 0)

                stage_q(t0, j, 0)
                stage_lin(t0, j, 1)
                split_tanh_hi(t0, j, 1)
                split_tanh_lo(t0, j, 1)
                stage_cube(t0, j, 1)
                stage_b(t0, j, 1)
                stage_lin(t0, j, 2)
                if more_cells:
                    cell_rz(t0, j + 1)

                stage_q(t0, j, 1)
                split_tanh_hi(t0, j, 2)
                split_tanh_lo(t0, j, 2)
                stage_cube(t0, j, 2)
                stage_b(t0, j, 2)
                end_lin(t0, j)
                end_q_part(t0, j)
                if more_cells:
                    cell_n_h(t0, j + 1)
                    cell_n_rh(t0, j + 1)
                    cell_n_in(t0, j + 1)

                stage_q(t0, j, 2)
                end_y(t0, j)
                split_tanh_hi(t0, j, 3)
                split_tanh_lo(t0, j, 3)
                stage_cube(t0, j, 3)
                if more_cells:
                    cell_z(t0, j + 1)
                end_base(t0, j)
                if more_cells:
                    cell_h(t0, j + 1)
                end_b(t0, j)
                if more_cells:
                    split_h_hi(t0, j + 1)
                end_b_clip(t0, j)
                if more_cells:
                    split_h_lo(t0, j + 1)

                stage_q(t0, j, 3)
                if more_steps:
                    split_tanh_hi(t0, j + 1, 0)
                    split_tanh_lo(t0, j + 1, 0)
            over_steps(dve, step)

        @block.gpsimd
        def _(pool):
            def tt(dst, a, b, op, done):
                nc.gpsimd.tensor_tensor(dst, a, b, op).then_inc(done, 1)

            def split_x_lo(t0, u):
                pool.wait_ge(xs_hi_ready, t0 + (u + 1))
                half = u // CHUNK % 2
                src = ring if isinstance(t0, int) and t0 + u < SLOTS else xs_raw
                tt(xs_lo[half][:, u % CHUNK, :, :].rearrange("p k b -> p (k b)"), src[:, u % SLOTS, :],
                   xs_hi[half][:, u % CHUNK, :, :].rearrange("p k b -> p (k b)").bitcast(F32), ALU.subtract, xs_lo_ready)

            def cell_d(t0, u):
                pool.wait_ge(n_gate_ready, t0 + (u + 1))
                wait(pool, h_ready, t0 + u)
                tt(h_minus_n[:, :], h[:, :], n_gate[:, :], ALU.subtract, h_minus_n_ready)

            def cell_x1(t0, u):
                pool.wait_ge(x_loaded[u % SLOTS], rounds(t0, u))
                pool.wait_ge(h_ready, t0 + (u + 1))
                tt(ring[:, u % SLOTS, :], ring[:, u % SLOTS, :], h[:, :], ALU.add, x1_ready)

            def cell_drive(t0, u):
                pool.wait_ge(x1_ready, t0 + (u + 1))
                wait(pool, e0_ready, t0 + u)
                tt(drive[:, :].rearrange("p (k b) -> p k b", b=B), ring[:, u % SLOTS, :].rearrange("p (k b) -> p k b", b=B),
                   rk_bias[:, :].unsqueeze(2).broadcast_to([P, K, B]), ALU.add, drive_ready)

            for u in range(2 * CHUNK):
                split_x_lo(0, u)
            pool.wait_ge(mags_ready, 1)
            nc.gpsimd.partition_all_reduce(allmags[:, :], mags[:, :], P, RED_MAX).then_inc(allmags_ready, 1)
            for u in range(2 * CHUNK, AHEAD):
                split_x_lo(0, u)
            pool.wait_ge(prep, 3)
            cell_d(0, 0)
            cell_x1(0, 0)
            cell_drive(0, 0)

            def stage_y(t0, j, s):
                wait(pool, q_ready, t0 * 4 + (4 * j + s))
                if s == 0:
                    wait(pool, b_ready, t0 + j)
                    b_s = b_state
                else:
                    pool.wait_ge(b_mid_ready, t0 * 3 + (3 * j + s))
                    b_s = b_mid
                tt(y[:, s, :], q[:, s, :], b_s[:, :], ALU.subtract, y_ready)

            def stage_base(t0, j, s):
                pool.wait_ge(lin_ready, t0 * 3 + (3 * j + s + 1))
                pool.wait_ge(cube_ready, t0 * 4 + (4 * j + s + 1))
                tt(base[:, s, :], lin[:, s, :], cube[:, :], ALU.subtract, base_ready)

            def step(t0, j):
                more_cells = before(t0, j + 1, T)
                stage_y(t0, j, 0)
                stage_base(t0, j, 0)
                if not isinstance(t0, int) or t0 + j >= 1:
                    tt(ring[:, (j - 1) % SLOTS, :], ring[:, (j - 1) % SLOTS, :], q[:, 0, :], ALU.add, out_ready)
                if splits_x(t0, j):
                    split_x_lo(t0, j + AHEAD)
                stage_y(t0, j, 1)
                stage_base(t0, j, 1)
                stage_y(t0, j, 2)
                pool.wait_ge(y_ready, t0 * 4 + (4 * j + 3))
                tt(y_sum[:, :], y[:, 1, :], y[:, 2, :], ALU.add, y12_ready)
                stage_base(t0, j, 2)
                pool.wait_ge(q_part_ready, t0 + (j + 1))
                pool.wait_ge(lin_end_ready, t0 + (j + 1))
                tt(q_sum[:, :], q_sum[:, :], lin_end[:, :], ALU.add, q_sum1_ready)
                if more_cells:
                    cell_d(t0, j + 1)
                pool.wait_ge(q_ready, t0 * 4 + (4 * j + 3))
                pool.wait_ge(q_sum1_ready, t0 + (j + 1))
                tt(q_sum[:, :], q_sum[:, :], q[:, 3, :], ALU.add, q_sum_ready)
                stage_y(t0, j, 3)
                pool.wait_ge(y_ready, t0 * 4 + (4 * j + 4))
                pool.wait_ge(y_part_ready, t0 + (j + 1))
                tt(y_sum[:, :], y_sum[:, :], y[:, 3, :], ALU.add, y_sum_ready)
                if more_cells:
                    cell_x1(t0, j + 1)
                    cell_drive(t0, j + 1)
            over_steps(pool, step)
            pool.wait_ge(q_ready, 4 * T)
            tt(ring[:, (T - 1) % SLOTS, :], ring[:, (T - 1) % SLOTS, :], q[:, 0, :], ALU.add, out_ready)


def kernel(x, cond_2048, L0_cond_W_ih, L0_cond_W_hh, L0_cond_b_ih, L0_cond_b_hh, L1_cond_coupling, L1_cond_bias):
    import numpy as np
    import concourse.bacc as bacc
    from concourse.bass_utils import run_bass_kernel_spmd

    x, cond, wih, whh, bih, bhh, cpl, bias = (np.asarray(a) for a in (
        x, cond_2048, L0_cond_W_ih, L0_cond_W_hh, L0_cond_b_ih, L0_cond_b_hh, L1_cond_coupling, L1_cond_bias))
    NB, T, D = x.shape
    K = D // 128

    def rows(w):
        return np.ascontiguousarray(w.reshape(K, 128, -1).transpose(1, 0, 2))

    arrays = {
        "x": np.ascontiguousarray(x.reshape(NB, T, K, 128).transpose(1, 3, 2, 0)).reshape(T, 128, K * NB),
        "cond": rows(cond.T).reshape(128, K * NB),
        "wih": rows(wih),
        "whh": rows(whh).reshape(128, K * 3 * D),
        "cpl": rows(cpl.T).reshape(128, K * D),
        "bih": np.ascontiguousarray(bih.reshape(-1, 128).T),
        "bhh": np.ascontiguousarray(bhh.reshape(-1, 128).T),
        "bias": np.ascontiguousarray(bias.reshape(-1, 128).T),
    }
    nc = bacc.Bacc("TRN2", target_bir_lowering=False, num_devices=1)
    args = [nc.dram_tensor(n + "_in", a.shape, mybir.dt.from_np(a.dtype), kind="ExternalInput").ap() for n, a in arrays.items()]
    out = nc.dram_tensor("out", (T, 128, K * NB), F32, kind="ExternalOutput").ap()
    gru_rk4_kernel(nc, *args, out)
    r = run_bass_kernel_spmd(nc, [{n + "_in": a for n, a in arrays.items()}], core_ids=[0])
    got = r.results[0]["out"].reshape(T, 128, K, NB).transpose(3, 0, 2, 1).reshape(NB, T, D)
    return np.ascontiguousarray(got)
```

```python
from contextlib import ExitStack

import concourse.bass as bass
from concourse import mybir

P = 128
F32 = mybir.dt.float32
F32R = mybir.dt.float32r
F16 = mybir.dt.float16
I32 = mybir.dt.int32
ALU = mybir.AluOpType
ACT = mybir.ActivationFunctionType
AX = mybir.AxisListType
RED_MAX = bass.bass_isa.ReduceOp.max

DT = 0.01
EPSILON = 0.08
ALPHA = 0.7
BETA = 0.8
CLAMP = 20.0

HALF = DT / 2
DRIFT = HALF * EPSILON
STAGE_DT = (HALF, HALF, DT, DT / 6)
B_DT = (DRIFT * BETA, DRIFT * BETA, 2 * DRIFT * BETA)
B_MAX = BETA * CLAMP - ALPHA
B_MIN = -BETA * CLAMP - ALPHA

UNROLL = 8
TAIL = 16
CHUNK = 4
SLOTS = 4
PIECES = 3
AHEAD = 9
TANH_SCALE = 2.0 ** 15


def gru_rk4_kernel(nc, x_in, cond_in, wih_in, whh_in, cpl_in, bih_in, bhh_in, bias_in, out):
    T, _, _ = x_in.shape
    K = 4
    B = 64
    KB = K * B
    M3 = 12
    assert T % UNROLL == 0 and T >= TAIL + 2 * UNROLL and UNROLL % (2 * CHUNK) == 0
    assert M3 == CHUNK * PIECES
    LAST_PIECE = T // CHUNK * M3
    FIRST_PIECES = M3 + PIECES

    ctx = ExitStack()
    with ctx:
        def sb(name, shape, dt=F32):
            return ctx.enter_context(nc.sbuf_tensor(name, shape, dt))

        def bank(name):
            return ctx.enter_context(nc.psum_tensor(name, [P, 512], F32))

        def sem(name):
            return ctx.enter_context(nc.semaphore(name))

        wih_hi = sb("wih_hi", [P, K, 1536], F32R)
        wih_lo = sb("wih_lo", [P, K, 1536], F32R)
        whh_hi = sb("whh_hi", [P, K, 1536], F16)
        whh_lo = sb("whh_lo", [P, K, 1536], F16)
        cpl_hi = sb("cpl_hi", [P, K, 512], F16)
        cpl_lo = sb("cpl_lo", [P, K, 512], F16)
        whh_raw = sb("whh_raw", [P, K * 1536])
        cpl_raw = sb("cpl_raw", [P, K * 512])
        gi = [sb(f"gi{i}", [P, M3, CHUNK, B]) for i in range(2)]
        ring = sb("ring", [P, SLOTS, KB])
        xs_raw = sb("xs_raw", [P, SLOTS, KB])
        xs_hi = [sb(f"xs_hi{i}", [P, CHUNK, K, B], F32R) for i in range(2)]
        xs_lo = [sb(f"xs_lo{i}", [P, CHUNK, K, B], F32R) for i in range(2)]

        bih = sb("bih", [P, M3])
        bhh = sb("bhh", [P, M3])
        gi_bias = sb("gi_bias", [P, M3])
        rk_bias = sb("rk_bias", [P, K])
        mags = sb("mags", [P, 3])
        allmags = sb("allmags", [P, 3])
        pow2 = sb("pow2", [P, 3])
        scale = sb("scale", [P, 3])
        gh_unscale = sb("gh_unscale", [P, 1])
        rk_unscale = sb("rk_unscale", [P, 4])

        q = sb("q", [P, 4, KB])
        q_raw = sb("q_raw", [P, KB])
        th = sb("th", [P, KB])
        th_hi = sb("th_hi", [P, KB], F16)
        th_lo = sb("th_lo", [P, KB], F16)
        sq = sb("sq", [P, KB])
        cube = sb("cube", [P, KB])
        b_state = sb("b_state", [P, KB])
        b_raw = sb("b_raw", [P, KB])
        b_mid = sb("b_mid", [P, KB])
        y = sb("y", [P, 4, KB])
        y_sum = sb("y_sum", [P, KB])
        drive = sb("drive", [P, KB])
        e = sb("e", [P, KB])
        lin = sb("lin", [P, 3, KB])
        lin_full = sb("lin_full", [P, KB])
        lin_end = sb("lin_end", [P, KB])
        base = sb("base", [P, 4, KB])
        q_sum = sb("q_sum", [P, KB])

        h = sb("h", [P, KB])
        h_hi = sb("h_hi", [P, KB], F16)
        h_lo = sb("h_lo", [P, KB], F16)
        rz_in = sb("rz_in", [P, 2 * KB])
        rz = sb("rz", [P, 2 * KB])
        n_h = sb("n_h", [P, KB])
        n_rh = sb("n_rh", [P, KB])
        n_in = sb("n_in", [P, KB])
        n_gate = sb("n_gate", [P, KB])
        h_minus_n = sb("h_minus_n", [P, KB])
        z_part = sb("z_part", [P, KB])

        ps_rk = bank("ps_rk")
        ps_rz = bank("ps_rz")
        ps_n = bank("ps_n")
        ps_gi = [bank(f"ps_gi{i}") for i in range(PIECES)]

        wih_loaded = [sem(f"wih_loaded{k}") for k in range(K)]
        whh_loaded = sem("whh_loaded")
        cpl_loaded = sem("cpl_loaded")
        cond_loaded = sem("cond_loaded")
        bias_loaded = sem("bias_loaded")
        x_loaded = [sem(f"x_loaded{i}") for i in range(SLOTS)]
        xs_loaded = [sem(f"xs_loaded{i}") for i in range(SLOTS)]
        stored = [sem(f"stored{i}") for i in range(SLOTS)]
        wih_hi_ready = sem("wih_hi_ready")
        wih_lo_ready = sem("wih_lo_ready")
        mags_ready = sem("mags_ready")
        allmags_ready = sem("allmags_ready")
        prep = sem("prep")
        whh_ready = sem("whh_ready")
        cpl_ready = sem("cpl_ready")
        gi_bias_ready = sem("gi_bias_ready")
        xs_hi_ready = sem("xs_hi_ready")
        xs_lo_ready = sem("xs_lo_ready")
        gi_summed = sem("gi_summed")
        gi_ready = sem("gi_ready")
        rz_summed = sem("rz_summed")
        n_summed = sem("n_summed")
        rz_in_ready = sem("rz_in_ready")
        rz_ready = sem("rz_ready")
        n_h_ready = sem("n_h_ready")
        n_rh_ready = sem("n_rh_ready")
        n_in_ready = sem("n_in_ready")
        n_gate_ready = sem("n_gate_ready")
        h_minus_n_ready = sem("h_minus_n_ready")
        z_part_ready = sem("z_part_ready")
        h_ready = sem("h_ready")
        h_hi_ready = sem("h_hi_ready")
        h_lo_ready = sem("h_lo_ready")
        x1_ready = sem("x1_ready")
        drive_ready = sem("drive_ready")
        rk_summed = sem("rk_summed")
        q_ready = sem("q_ready")
        q_raw_ready = sem("q_raw_ready")
        th_ready = sem("th_ready")
        th_hi_ready = sem("th_hi_ready")
        th_lo_ready = sem("th_lo_ready")
        sq_ready = sem("sq_ready")
        cube_ready = sem("cube_ready")
        y_ready = sem("y_ready")
        b_mid_ready = sem("b_mid_ready")
        b_raw_ready = sem("b_raw_ready")
        b_ready = sem("b_ready")
        e_ready = sem("e_ready")
        lin_ready = sem("lin_ready")
        lin_full_ready = sem("lin_full_ready")
        lin_end0_ready = sem("lin_end0_ready")
        lin_end_ready = sem("lin_end_ready")
        base0_ready = sem("base0_ready")
        base_ready = sem("base_ready")
        base3_ready = sem("base3_ready")
        y12_ready = sem("y12_ready")
        y_part_ready = sem("y_part_ready")
        y_sum_ready = sem("y_sum_ready")
        q_part_ready = sem("q_part_ready")
        q_sum1_ready = sem("q_sum1_ready")
        q_sum_ready = sem("q_sum_ready")
        out_ready = sem("out_ready")

        def wait(eng, s, value):
            if not isinstance(value, int) or value > 0:
                eng.wait_ge(s, value)

        def over_steps(eng, step):
            for j in range(UNROLL):
                step(0, j)
            with eng.Fori(UNROLL, T - TAIL - UNROLL + 1, UNROLL) as t0:
                for j in range(UNROLL):
                    step(t0, j)
            for j in range(TAIL):
                step(T - TAIL, j)

        def before(t0, j, limit):
            return not isinstance(t0, int) or t0 + j < limit

        def rounds(t0, j):
            return t0 * (16 // SLOTS) + 16 * (j // SLOTS + 1)

        def x_at(dram, t0, j):
            if isinstance(t0, int):
                return dram[t0 + j, :, :]
            return dram[bass.ds(t0 + j, 1), :, :].rearrange("t p n -> p (t n)")

        def splits_x(t0, j):
            return before(t0, j + AHEAD, T)

        block = ctx.enter_context(nc.Block())

        @block.sync
        def _(sp):
            sp.dma_start(bih[:, :], bih_in).then_inc(bias_loaded, 16)
            sp.dma_start(bhh[:, :], bhh_in).then_inc(bias_loaded, 16)
            sp.dma_start(rk_bias[:, :], bias_in).then_inc(bias_loaded, 16)
            for u in range(SLOTS):
                sp.dma_start(ring[:, u, :], x_at(x_in, 0, u)).then_inc(x_loaded[u], 16)
            for k in range(K):
                raw = gi[k // 2][:, :, :, :].rearrange("p m j b -> p (m j b)")
                sp.dma_start(raw[:, k % 2 * 1536:(k % 2 + 1) * 1536], wih_in[:, k, :]).then_inc(wih_loaded[k], 16)
            for u in range(SLOTS, 2 * SLOTS):
                sp.dma_start(xs_raw[:, u % SLOTS, :], x_at(x_in, 0, u)).then_inc(xs_loaded[u % SLOTS], 16)
            sp.dma_start(q[:, 0, :], cond_in).then_inc(cond_loaded, 16)
            sp.dma_start(h[:, :], cond_in).then_inc(cond_loaded, 16)
            sp.dma_start(whh_raw[:, :], whh_in).then_inc(whh_loaded, 16)
            sp.dma_start(cpl_raw[:, :], cpl_in).then_inc(cpl_loaded, 16)

            def refill_xs(t0, u):
                sp.wait_ge(xs_lo_ready, t0 + (u - SLOTS + 1))
                sp.dma_start(xs_raw[:, u % SLOTS, :], x_at(x_in, t0, u)).then_inc(xs_loaded[u % SLOTS], 16)

            for u in range(2 * SLOTS, AHEAD + SLOTS):
                refill_xs(0, u)

            def step(t0, j):
                if before(t0, j + AHEAD + SLOTS, T):
                    refill_xs(t0, j + AHEAD + SLOTS)
                if (not isinstance(t0, int) or t0 + j >= 1) and before(t0, j - 1 + SLOTS, T):
                    slot = (j - 1) % SLOTS
                    sp.wait_ge(stored[slot], rounds(t0, j - 1))
                    sp.dma_start(ring[:, slot, :], x_at(x_in, t0, j - 1 + SLOTS)).then_inc(x_loaded[slot], 16)
                sp.wait_ge(out_ready, t0 + (j + 1))
                sp.dma_start(x_at(out, t0, j), ring[:, j % SLOTS, :]).then_inc(stored[j % SLOTS], 16)
            over_steps(sp, step)
            for s in stored:
                sp.wait_ge(s, 16 * (T // SLOTS))

        @block.tensor
        def _(pe):
            def product(ps, cols, w_hi, w_lo, w_cols, v_hi, v_lo, done, first=0, end=None, before_lo=None):
                count = 3 * cols * K
                for n in range(first, count if end is None else end):
                    part, r = divmod(n, cols * K)
                    m, k = divmod(r, K)
                    if part == 2 and r == 0 and before_lo is not None:
                        before_lo()
                    w = w_lo if part == 0 else w_hi
                    v = v_lo if part == 2 else v_hi
                    mm = nc.tensor.matmul(ps[:, m * B:(m + 1) * B], w[:, k, w_cols + m * P:w_cols + (m + 1) * P],
                                          v[:, k * B:(k + 1) * B], start=(n == 0), stop=(n == count - 1),
                                          skip_group_check=True)
                    if n == count - 1:
                        mm.then_inc(done, 1)

            def coupling(t0, j, s):
                pe.wait_ge(th_hi_ready, t0 * 4 + (4 * j + s + 1))
                product(ps_rk, K, cpl_hi, cpl_lo, 0, th_hi, th_lo, rk_summed,
                        before_lo=lambda: pe.wait_ge(th_lo_ready, t0 * 4 + (4 * j + s + 1)))

            def gates_rz(t0, j, first=0, end=None):
                if first == 0:
                    pe.wait_ge(h_lo_ready, t0 + (j + 1))
                product(ps_rz, 2 * K, whh_hi, whh_lo, 0, h_hi, h_lo, rz_summed, first, end)

            def gates_n(t0, j):
                pe.wait_ge(h_lo_ready, t0 + (j + 1))
                product(ps_n, K, whh_hi, whh_lo, 8 * P, h_hi, h_lo, n_summed)

            def project(t0, first, offset, lo, hi):
                for n in range(lo, hi):
                    i, r = divmod(n, 3 * K)
                    k, part = divmod(r, 3)
                    g = first + i
                    m = g % M3
                    par = g // M3 % 2
                    if r == 0:
                        wait(pe, gi_ready, t0 * 3 + (g - PIECES + 1))
                    if part == 2:
                        w, v = wih_lo, xs_hi[par]
                    else:
                        w, v = wih_hi, (xs_hi, xs_lo)[part][par]
                    last = nc.tensor.matmul(ps_gi[i][:, 0:CHUNK * B].rearrange("p (j b) -> p j b", j=CHUNK),
                                            w[:, k, m * P:(m + 1) * P], v[:, :, k, :],
                                            start=(r == 0), stop=(r == 3 * K - 1))
                    if r == 3 * K - 1:
                        last.then_inc(gi_summed, 1)

            pe.wait_ge(wih_hi_ready, K)
            pe.wait_ge(wih_lo_ready, K)
            for c in range(FIRST_PIECES // PIECES):
                pe.wait_ge(xs_hi_ready, CHUNK * (1 + c * PIECES // M3))
                pe.wait_ge(xs_lo_ready, CHUNK * (1 + c * PIECES // M3))
                project(0, c * PIECES, 0, 0, PIECES * 3 * K)
            pe.wait_ge(whh_ready, 2)
            gates_rz(0, 0)
            gates_n(0, 0)
            pe.wait_ge(cpl_ready, 2)

            def step(t0, j):
                more_cells = before(t0, j + 1, T)
                first = FIRST_PIECES + 3 * j
                more_pieces = not isinstance(t0, int) or t0 * 3 + first < LAST_PIECE
                coupling(t0, j, 0)
                if more_cells:
                    gates_rz(t0, j + 1, 0, 72)
                coupling(t0, j, 1)
                if more_cells:
                    gates_rz(t0, j + 1, 72)
                    gates_n(t0, j + 1)
                coupling(t0, j, 2)
                if more_pieces:
                    pe.wait_ge(xs_hi_ready, t0 + CHUNK * (first // M3 + 1))
                    pe.wait_ge(xs_lo_ready, t0 + CHUNK * (first // M3 + 1))
                    project(t0, first, j, 0, 18)
                coupling(t0, j, 3)
                if more_pieces:
                    project(t0, first, j, 18, 36)
            over_steps(pe, step)

        @block.scalar
        def _(act):
            def split_x_hi(t0, u):
                if isinstance(t0, int) and t0 + u < SLOTS:
                    act.wait_ge(x_loaded[u], 16)
                    src = ring
                else:
                    act.wait_ge(xs_loaded[u % SLOTS], rounds(t0, u - SLOTS))
                    src = xs_raw
                nc.scalar.activation(xs_hi[u // CHUNK % 2][:, u % CHUNK, :, :].rearrange("p k b -> p (k b)"),
                                     src[:, u % SLOTS, :], ACT.Copy).then_inc(xs_hi_ready, 1)

            def store_gi(t0, g):
                act.wait_ge(gi_summed, t0 * 3 + (g + 1))
                m = g % M3
                nc.scalar.activation(gi[g // M3 % 2][:, m, :, :].rearrange("p j b -> p (j b)"),
                                     ps_gi[g % PIECES][:, 0:CHUNK * B], ACT.Identity,
                                     bias=gi_bias[:, m:m + 1], scale=1.0).then_inc(gi_ready, 1)

            def gate_rz(t0, j):
                act.wait_ge(rz_in_ready, t0 + (j + 1))
                nc.scalar.activation(rz[:, :], rz_in[:, :], ACT.Tanh, scale=0.5).then_inc(rz_ready, 1)

            def split_h_hi(t0, u):
                act.wait_ge(h_ready, t0 + (u + 1))
                nc.scalar.activation(h_hi[:, :], h[:, :], ACT.Copy, scale=scale[:, 2:3]).then_inc(h_hi_ready, 1)

            def gate_n(t0, j):
                act.wait_ge(n_in_ready, t0 + (j + 1))
                nc.scalar.activation(n_gate[:, :], n_in[:, :], ACT.Tanh).then_inc(n_gate_ready, 1)

            def tanh(t0, j, s):
                wait(act, q_ready, t0 * 4 + (4 * j + s))
                wait(act, th_lo_ready, t0 * 4 + (4 * j + s))
                nc.scalar.activation(th[:, :], q[:, s, :], ACT.Tanh).then_inc(th_ready, 1)

            def tanh_hi(t0, j, s):
                act.wait_ge(th_ready, t0 * 4 + (4 * j + s + 1))
                nc.scalar.activation(th_hi[:, :], th[:, :], ACT.Copy, scale=TANH_SCALE).then_inc(th_hi_ready, 1)

            def square(t0, j, s):
                wait(act, cube_ready, t0 * 4 + (4 * j + s))
                nc.scalar.activation(sq[:, :], q[:, s, :], ACT.Square,
                                     scale=(STAGE_DT[s] / 3) ** 0.5).then_inc(sq_ready, 1)

            for u in range(CHUNK):
                split_x_hi(0, u)
            for k in range(K):
                act.wait_ge(wih_loaded[k], 16)
                raw = gi[k // 2][:, :, :, :].rearrange("p m j b -> p (m j b)")
                nc.scalar.activation(wih_hi[:, k, :], raw[:, k % 2 * 1536:(k % 2 + 1) * 1536],
                                     ACT.Copy).then_inc(wih_hi_ready, 1)
            for u in range(CHUNK, 2 * CHUNK):
                split_x_hi(0, u)
            act.wait_ge(gi_bias_ready, 2)
            act.wait_ge(wih_lo_ready, K)
            for g in range(FIRST_PIECES):
                store_gi(0, g)
            for u in range(2 * CHUNK, AHEAD):
                split_x_hi(0, u)
            act.wait_ge(prep, 14)
            gate_rz(0, 0)
            gate_n(0, 0)
            split_h_hi(0, 0)

            def step(t0, j):
                more_cells = before(t0, j + 1, T)
                first = FIRST_PIECES + 3 * j
                more_pieces = not isinstance(t0, int) or t0 * 3 + first < LAST_PIECE
                late = (not isinstance(t0, int) or t0 + j >= 1) and (not isinstance(t0, int) or t0 * 3 + first - PIECES < LAST_PIECE)
                tanh(t0, j, 0)
                tanh_hi(t0, j, 0)
                square(t0, j, 0)
                if late:
                    store_gi(t0, first - 2)
                tanh(t0, j, 1)
                tanh_hi(t0, j, 1)
                square(t0, j, 1)
                tanh(t0, j, 2)
                tanh_hi(t0, j, 2)
                square(t0, j, 2)
                if splits_x(t0, j):
                    split_x_hi(t0, j + AHEAD)
                if more_cells:
                    gate_rz(t0, j + 1)
                if late:
                    store_gi(t0, first - 1)
                tanh(t0, j, 3)
                if more_cells:
                    gate_n(t0, j + 1)
                tanh_hi(t0, j, 3)
                square(t0, j, 3)
                if more_pieces:
                    store_gi(t0, first)
                if more_cells:
                    split_h_hi(t0, j + 1)
            over_steps(act, step)

        @block.vector
        def _(dve):
            def fma(dst, a, c, b, done, op1=ALU.add):
                nc.vector.scalar_tensor_tensor(out=dst, in0=a, scalar=c, in1=b, op0=ALU.mult, op1=op1).then_inc(done, 1)

            def cell_rz(t0, u):
                dve.wait_ge(rz_summed, t0 + (u + 1))
                dve.wait_ge(gi_ready, t0 * 3 + (M3 * (u // CHUNK) + 2 * K))
                blocks = gi[u // CHUNK % 2][:, 0:8, u % CHUNK, :]
                fma(rz_in[:, :].rearrange("p (m b) -> p m b", b=B), ps_rz[:, :].rearrange("p (m b) -> p m b", b=B),
                    gh_unscale[:, 0:1], blocks, rz_in_ready)

            def cell_n_h(t0, u):
                dve.wait_ge(n_summed, t0 + (u + 1))
                fma(n_h[:, :].rearrange("p (m b) -> p m b", b=B), ps_n[:, 0:KB].rearrange("p (m b) -> p m b", b=B),
                    gh_unscale[:, 0:1], bhh[:, 8:12].unsqueeze(2).broadcast_to([P, K, B]), n_h_ready)

            def cell_n_rh(t0, u):
                dve.wait_ge(rz_ready, t0 + (u + 1))
                dve.wait_ge(n_h_ready, t0 + (u + 1))
                nc.vector.scalar_tensor_tensor(out=n_rh[:, :], in0=rz[:, 0:KB], scalar=1.0, in1=n_h[:, :],
                                               op0=ALU.add, op1=ALU.mult).then_inc(n_rh_ready, 1)

            def cell_n_in(t0, u):
                dve.wait_ge(n_rh_ready, t0 + (u + 1))
                dve.wait_ge(gi_ready, t0 * 3 + M3 * (u // CHUNK + 1))
                fma(n_in[:, :].rearrange("p (m b) -> p m b", b=B), n_rh[:, :].rearrange("p (m b) -> p m b", b=B),
                    0.5, gi[u // CHUNK % 2][:, 8:12, u % CHUNK, :], n_in_ready)

            def cell_z(t0, u):
                dve.wait_ge(h_minus_n_ready, t0 + (u + 1))
                nc.vector.scalar_tensor_tensor(out=z_part[:, :], in0=rz[:, KB:2 * KB], scalar=1.0, in1=h_minus_n[:, :],
                                               op0=ALU.add, op1=ALU.mult).then_inc(z_part_ready, 1)

            def cell_h(t0, u):
                dve.wait_ge(z_part_ready, t0 + (u + 1))
                wait(dve, x1_ready, t0 + u)
                fma(h[:, :], z_part[:, :], 0.5, n_gate[:, :], h_ready)

            def split_h_lo(t0, u):
                dve.wait_ge(h_hi_ready, t0 + (u + 2))
                fma(h_lo[:, :], h[:, :], scale[:, 2:3], h_hi[:, :], h_lo_ready, ALU.subtract)

            for k in range(K):
                dve.wait_ge(wih_hi_ready, k + 1)
                raw = gi[k // 2][:, :, :, :].rearrange("p m j b -> p (m j b)")
                nc.vector.tensor_tensor(wih_lo[:, k, :], raw[:, k % 2 * 1536:(k % 2 + 1) * 1536],
                                        wih_hi[:, k, :].bitcast(F32), ALU.subtract).then_inc(wih_lo_ready, 1)
            dve.wait_ge(bias_loaded, 48)
            nc.vector.tensor_tensor(gi_bias[:, 0:8], bih[:, 0:8], bhh[:, 0:8], ALU.add).then_inc(gi_bias_ready, 1)
            nc.vector.tensor_copy(gi_bias[:, 8:12], bih[:, 8:12]).then_inc(gi_bias_ready, 1)
            nc.vector.tensor_scalar(rk_bias[:, :], rk_bias[:, :], -ALPHA / BETA, None, op0=ALU.add).then_inc(prep, 1)
            dve.wait_ge(cond_loaded, 32)
            nc.vector.tensor_scalar(b_state[:, :], q[:, 0, :], BETA, -ALPHA, op0=ALU.mult, op1=ALU.add).then_inc(prep, 1)
            nc.vector.tensor_reduce(mags[:, 2:3], q[:, 0, :], AX.X, ALU.max, apply_absolute_value=True).then_inc(prep, 1)
            dve.wait_ge(whh_loaded, 16)
            nc.vector.tensor_reduce(mags[:, 0:1], whh_raw[:, :], AX.X, ALU.max, apply_absolute_value=True).then_inc(prep, 1)
            dve.wait_ge(cpl_loaded, 16)
            nc.vector.tensor_reduce(mags[:, 1:2], cpl_raw[:, :], AX.X, ALU.max, apply_absolute_value=True).then_inc(mags_ready, 1)
            dve.wait_ge(allmags_ready, 1)
            dve.wait_ge(mags_ready, 1)
            nc.vector.tensor_scalar(mags[:, 0:2], allmags[:, 0:2], 2.0 ** -100, None, op0=ALU.max).then_inc(prep, 1)
            nc.vector.tensor_scalar(mags[:, 2:3], allmags[:, 2:3], 1.0, None, op0=ALU.max).then_inc(prep, 1)
            dve.wait_ge(prep, 6)
            nc.vector.tensor_scalar(pow2[:, :].bitcast(I32), mags[:, :].bitcast(I32), 0x7F800000, None,
                                    op0=ALU.bitwise_and).then_inc(prep, 1)
            dve.wait_ge(prep, 7)
            nc.vector.tensor_scalar(pow2[:, :], pow2[:, :], 2.0 ** -14, None, op0=ALU.mult).then_inc(prep, 1)
            dve.wait_ge(prep, 8)
            nc.vector.reciprocal(scale[:, :], pow2[:, :]).then_inc(prep, 1)
            nc.vector.tensor_tensor(gh_unscale[:, :], pow2[:, 0:1], pow2[:, 2:3], ALU.mult).then_inc(prep, 1)
            for s in range(4):
                nc.vector.tensor_scalar(rk_unscale[:, s:s + 1], pow2[:, 1:2], STAGE_DT[s] / TANH_SCALE, None,
                                        op0=ALU.mult).then_inc(prep, 1)
            dve.wait_ge(prep, 14)
            nc.vector.tensor_scalar(h_hi[:, :], h[:, :], scale[:, 2:3], None, op0=ALU.mult).then_inc(h_hi_ready, 1)
            flat = [w[:, :, :].rearrange("p k n -> p (k n)") for w in (whh_hi, whh_lo, cpl_hi, cpl_lo)]
            nc.vector.tensor_scalar(flat[0], whh_raw[:, :], scale[:, 0:1], None, op0=ALU.mult).then_inc(whh_ready, 1)
            split_h_lo(0, -1)
            dve.wait_ge(whh_ready, 1)
            fma(flat[1], whh_raw[:, :], scale[:, 0:1], flat[0], whh_ready, ALU.subtract)
            nc.vector.tensor_scalar(flat[2], cpl_raw[:, :], scale[:, 1:2], None, op0=ALU.mult).then_inc(cpl_ready, 1)
            dve.wait_ge(cpl_ready, 1)
            fma(flat[3], cpl_raw[:, :], scale[:, 1:2], flat[2], cpl_ready, ALU.subtract)

            def stage_cube(t0, j, s):
                dve.wait_ge(sq_ready, t0 * 4 + (4 * j + s + 1))
                wait(dve, q_ready, t0 * 4 + (4 * j + s))
                if s == 0:
                    wait(dve, base3_ready, t0 + j)
                elif s == 1:
                    dve.wait_ge(base0_ready, t0 + (j + 1))
                else:
                    dve.wait_ge(base_ready, t0 * 2 + (2 * j + s - 1))
                nc.vector.scalar_tensor_tensor(out=cube[:, :], in0=sq[:, :], scalar=-STAGE_DT[s], in1=q[:, s, :],
                                               op0=ALU.add, op1=ALU.mult).then_inc(cube_ready, 1)

            def split_tanh_lo(t0, j, s):
                dve.wait_ge(th_hi_ready, t0 * 4 + (4 * j + s + 1))
                fma(th_lo[:, :], th[:, :], TANH_SCALE, th_hi[:, :], th_lo_ready, ALU.subtract)

            def stage_q(t0, j, s):
                dve.wait_ge(rk_summed, t0 * 4 + (4 * j + s + 1))
                if s < 3:
                    if s == 0:
                        dve.wait_ge(base0_ready, t0 + (j + 1))
                    else:
                        dve.wait_ge(base_ready, t0 * 2 + (2 * j + s))
                    fma(q[:, s + 1, :], ps_rk[:, 0:KB], rk_unscale[:, s:s + 1], base[:, s, :], q_ready)
                else:
                    dve.wait_ge(base3_ready, t0 + (j + 1))
                    fma(q_raw[:, :], ps_rk[:, 0:KB], rk_unscale[:, s:s + 1], base[:, s, :], q_raw_ready)
                    dve.wait_ge(q_raw_ready, t0 + (j + 1))
                    nc.vector.tensor_scalar(q[:, 0, :], q_raw[:, :], -CLAMP, CLAMP, op0=ALU.max, op1=ALU.min).then_inc(q_ready, 1)

            def start_e(t0, j):
                dve.wait_ge(drive_ready, t0 + (j + 1))
                wait(dve, b_ready, t0 + j)
                fma(e[:, :], b_state[:, :], -1.0 / BETA, drive[:, :], e_ready)

            def start_lin0(t0, j):
                dve.wait_ge(e_ready, t0 + (j + 1))
                wait(dve, q_ready, t0 * 4 + 4 * j)
                fma(lin[:, 0, :], e[:, :], HALF, q[:, 0, :], lin_ready)

            def start_lin_full(t0, j):
                dve.wait_ge(e_ready, t0 + (j + 1))
                fma(lin_full[:, :], e[:, :], DT, q[:, 0, :], lin_full_ready)

            def start_lin_end(t0, j):
                dve.wait_ge(e_ready, t0 + (j + 1))
                fma(lin_end[:, :], e[:, :], HALF, q[:, 0, :], lin_end0_ready, ALU.subtract)

            def stage0_base(t0, j):
                dve.wait_ge(lin_ready, t0 * 3 + (3 * j + 1))
                dve.wait_ge(cube_ready, t0 * 4 + (4 * j + 1))
                nc.vector.tensor_tensor(base[:, 0, :], lin[:, 0, :], cube[:, :], ALU.subtract).then_inc(base0_ready, 1)

            def stage_b(t0, j, s):
                dve.wait_ge(y_ready, t0 * 4 + (4 * j + s + 1))
                fma(b_mid[:, :], y[:, s, :], B_DT[s], b_state[:, :], b_mid_ready)

            def stage_lin(t0, j, s):
                dve.wait_ge(y_ready, t0 * 4 + (4 * j + s))
                if s == 1:
                    dve.wait_ge(lin_ready, t0 * 3 + (3 * j + 1))
                    fma(lin[:, 1, :], y[:, 0, :], -HALF * DRIFT, lin[:, 0, :], lin_ready)
                else:
                    dve.wait_ge(lin_full_ready, t0 + (j + 1))
                    fma(lin[:, 2, :], y[:, 1, :], -DT * DRIFT, lin_full[:, :], lin_ready)

            def end_lin(t0, j):
                dve.wait_ge(y_ready, t0 * 4 + (4 * j + 3))
                dve.wait_ge(lin_end0_ready, t0 + (j + 1))
                fma(lin_end[:, :], y[:, 2, :], -DT * DRIFT, lin_end[:, :], lin_end_ready)

            def end_q_part(t0, j):
                dve.wait_ge(q_ready, t0 * 4 + (4 * j + 2))
                fma(q_sum[:, :], q[:, 2, :], 2.0, q[:, 1, :], q_part_ready)

            def end_y(t0, j):
                dve.wait_ge(y12_ready, t0 + (j + 1))
                fma(y_sum[:, :], y_sum[:, :], 2.0, y[:, 0, :], y_part_ready)

            def end_base(t0, j):
                dve.wait_ge(q_sum_ready, t0 + (j + 1))
                dve.wait_ge(cube_ready, t0 * 4 + (4 * j + 4))
                fma(base[:, 3, :], q_sum[:, :], 1.0 / 3, cube[:, :], base3_ready, ALU.subtract)

            def end_b(t0, j):
                dve.wait_ge(y_sum_ready, t0 + (j + 1))
                fma(b_raw[:, :], y_sum[:, :], DRIFT * BETA / 3, b_state[:, :], b_raw_ready)

            def end_b_clip(t0, j):
                dve.wait_ge(b_raw_ready, t0 + (j + 1))
                nc.vector.tensor_scalar(b_state[:, :], b_raw[:, :], B_MIN, B_MAX, op0=ALU.max, op1=ALU.min).then_inc(b_ready, 1)

            cell_rz(0, 0)
            cell_n_h(0, 0)
            cell_n_rh(0, 0)
            cell_n_in(0, 0)
            cell_z(0, 0)
            cell_h(0, 0)
            split_h_lo(0, 0)
            start_e(0, 0)
            split_tanh_lo(0, 0, 0)

            def step(t0, j):
                more_cells = before(t0, j + 1, T)
                stage_cube(t0, j, 0)
                start_lin0(t0, j)
                stage0_base(t0, j)

                stage_q(t0, j, 0)
                stage_b(t0, j, 0)
                start_lin_end(t0, j)
                stage_lin(t0, j, 1)
                split_tanh_lo(t0, j, 1)
                stage_cube(t0, j, 1)
                start_lin_full(t0, j)
                stage_lin(t0, j, 2)
                stage_b(t0, j, 1)

                stage_q(t0, j, 1)
                if more_cells:
                    cell_rz(t0, j + 1)
                end_lin(t0, j)
                split_tanh_lo(t0, j, 2)
                stage_cube(t0, j, 2)
                if more_cells:
                    cell_n_h(t0, j + 1)
                end_q_part(t0, j)
                if more_cells:
                    cell_n_rh(t0, j + 1)

                stage_q(t0, j, 2)
                if more_cells:
                    cell_n_in(t0, j + 1)
                end_y(t0, j)
                stage_b(t0, j, 2)
                split_tanh_lo(t0, j, 3)
                stage_cube(t0, j, 3)
                if more_cells:
                    cell_z(t0, j + 1)
                end_base(t0, j)
                if more_cells:
                    cell_h(t0, j + 1)

                stage_q(t0, j, 3)
                end_b(t0, j)
                end_b_clip(t0, j)
                if more_cells:
                    split_h_lo(t0, j + 1)
                    start_e(t0, j + 1)
                    split_tanh_lo(t0, j + 1, 0)
            over_steps(dve, step)

        @block.gpsimd
        def _(pool):
            def tt(dst, a, b, op, done):
                nc.gpsimd.tensor_tensor(dst, a, b, op).then_inc(done, 1)

            def split_x_lo(t0, u):
                pool.wait_ge(xs_hi_ready, t0 + (u + 1))
                half = u // CHUNK % 2
                src = ring if isinstance(t0, int) and t0 + u < SLOTS else xs_raw
                tt(xs_lo[half][:, u % CHUNK, :, :].rearrange("p k b -> p (k b)"), src[:, u % SLOTS, :],
                   xs_hi[half][:, u % CHUNK, :, :].rearrange("p k b -> p (k b)").bitcast(F32), ALU.subtract, xs_lo_ready)

            def cell_d(t0, u):
                pool.wait_ge(n_gate_ready, t0 + (u + 1))
                wait(pool, h_ready, t0 + u)
                tt(h_minus_n[:, :], h[:, :], n_gate[:, :], ALU.subtract, h_minus_n_ready)

            def cell_x1(t0, u):
                pool.wait_ge(x_loaded[u % SLOTS], rounds(t0, u))
                pool.wait_ge(h_ready, t0 + (u + 1))
                tt(ring[:, u % SLOTS, :], ring[:, u % SLOTS, :], h[:, :], ALU.add, x1_ready)

            def cell_drive(t0, u):
                pool.wait_ge(x1_ready, t0 + (u + 1))
                wait(pool, e_ready, t0 + u)
                tt(drive[:, :].rearrange("p (k b) -> p k b", b=B), ring[:, u % SLOTS, :].rearrange("p (k b) -> p k b", b=B),
                   rk_bias[:, :].unsqueeze(2).broadcast_to([P, K, B]), ALU.add, drive_ready)

            for u in range(2 * CHUNK):
                split_x_lo(0, u)
            pool.wait_ge(mags_ready, 1)
            nc.gpsimd.partition_all_reduce(allmags[:, :], mags[:, :], P, RED_MAX).then_inc(allmags_ready, 1)
            for u in range(2 * CHUNK, AHEAD):
                split_x_lo(0, u)
            pool.wait_ge(prep, 3)
            cell_d(0, 0)
            cell_x1(0, 0)
            cell_drive(0, 0)

            def stage_y(t0, j, s):
                wait(pool, q_ready, t0 * 4 + (4 * j + s))
                if s == 0:
                    wait(pool, b_ready, t0 + j)
                    b_s = b_state
                else:
                    pool.wait_ge(b_mid_ready, t0 * 3 + (3 * j + s))
                    b_s = b_mid
                tt(y[:, s, :], q[:, s, :], b_s[:, :], ALU.subtract, y_ready)

            def stage_base(t0, j, s):
                pool.wait_ge(lin_ready, t0 * 3 + (3 * j + s + 1))
                pool.wait_ge(cube_ready, t0 * 4 + (4 * j + s + 1))
                tt(base[:, s, :], lin[:, s, :], cube[:, :], ALU.subtract, base_ready)

            def step(t0, j):
                more_cells = before(t0, j + 1, T)
                if not isinstance(t0, int) or t0 + j >= 1:
                    pool.wait_ge(q_ready, t0 * 4 + 4 * j)
                    tt(ring[:, (j - 1) % SLOTS, :], ring[:, (j - 1) % SLOTS, :], q[:, 0, :], ALU.add, out_ready)
                stage_y(t0, j, 0)
                stage_y(t0, j, 1)
                stage_base(t0, j, 1)
                stage_y(t0, j, 2)
                pool.wait_ge(y_ready, t0 * 4 + (4 * j + 3))
                tt(y_sum[:, :], y[:, 1, :], y[:, 2, :], ALU.add, y12_ready)
                stage_base(t0, j, 2)
                pool.wait_ge(q_part_ready, t0 + (j + 1))
                pool.wait_ge(lin_end_ready, t0 + (j + 1))
                tt(q_sum[:, :], q_sum[:, :], lin_end[:, :], ALU.add, q_sum1_ready)
                pool.wait_ge(q_ready, t0 * 4 + (4 * j + 3))
                pool.wait_ge(q_sum1_ready, t0 + (j + 1))
                tt(q_sum[:, :], q_sum[:, :], q[:, 3, :], ALU.add, q_sum_ready)
                if more_cells:
                    cell_d(t0, j + 1)
                stage_y(t0, j, 3)
                pool.wait_ge(y_ready, t0 * 4 + (4 * j + 4))
                pool.wait_ge(y_part_ready, t0 + (j + 1))
                tt(y_sum[:, :], y_sum[:, :], y[:, 3, :], ALU.add, y_sum_ready)
                if more_cells:
                    cell_x1(t0, j + 1)
                    cell_drive(t0, j + 1)
                if splits_x(t0, j):
                    split_x_lo(t0, j + AHEAD)
            over_steps(pool, step)
            pool.wait_ge(q_ready, 4 * T)
            tt(ring[:, (T - 1) % SLOTS, :], ring[:, (T - 1) % SLOTS, :], q[:, 0, :], ALU.add, out_ready)


def kernel(x, cond_2048, L0_cond_W_ih, L0_cond_W_hh, L0_cond_b_ih, L0_cond_b_hh, L1_cond_coupling, L1_cond_bias):
    import numpy as np
    import concourse.bacc as bacc
    from concourse.bass_utils import run_bass_kernel_spmd

    x, cond, wih, whh, bih, bhh, cpl, bias = (np.asarray(a) for a in (
        x, cond_2048, L0_cond_W_ih, L0_cond_W_hh, L0_cond_b_ih, L0_cond_b_hh, L1_cond_coupling, L1_cond_bias))
    NB, T, D = x.shape
    K = D // 128

    def rows(w):
        return np.ascontiguousarray(w.reshape(K, 128, -1).transpose(1, 0, 2))

    arrays = {
        "x": np.ascontiguousarray(x.reshape(NB, T, K, 128).transpose(1, 3, 2, 0)).reshape(T, 128, K * NB),
        "cond": rows(cond.T).reshape(128, K * NB),
        "wih": rows(wih),
        "whh": rows(whh).reshape(128, K * 3 * D),
        "cpl": rows(cpl.T).reshape(128, K * D),
        "bih": np.ascontiguousarray(bih.reshape(-1, 128).T),
        "bhh": np.ascontiguousarray(bhh.reshape(-1, 128).T),
        "bias": np.ascontiguousarray(bias.reshape(-1, 128).T),
    }
    nc = bacc.Bacc("TRN2", target_bir_lowering=False, num_devices=1)
    args = [nc.dram_tensor(n + "_in", a.shape, mybir.dt.from_np(a.dtype), kind="ExternalInput").ap() for n, a in arrays.items()]
    out = nc.dram_tensor("out", (T, 128, K * NB), F32, kind="ExternalOutput").ap()
    gru_rk4_kernel(nc, *args, out)
    r = run_bass_kernel_spmd(nc, [{n + "_in": a for n, a in arrays.items()}], core_ids=[0])
    got = r.results[0]["out"].reshape(T, 128, K, NB).transpose(3, 0, 2, 1).reshape(NB, T, D)
    return np.ascontiguousarray(got)
```

```python
from contextlib import ExitStack

import concourse.bass as bass
from concourse import mybir

P = 128
F32 = mybir.dt.float32
F32R = mybir.dt.float32r
F16 = mybir.dt.float16
I32 = mybir.dt.int32
ALU = mybir.AluOpType
ACT = mybir.ActivationFunctionType
AX = mybir.AxisListType
RED_MAX = bass.bass_isa.ReduceOp.max

DT = 0.01
EPSILON = 0.08
ALPHA = 0.7
BETA = 0.8
CLAMP = 20.0

HALF = DT / 2
DRIFT = HALF * EPSILON
STAGE_DT = (HALF, HALF, DT, DT / 6)
B_DT = (DRIFT * BETA, DRIFT * BETA, 2 * DRIFT * BETA)
B_MAX = BETA * CLAMP - ALPHA
B_MIN = -BETA * CLAMP - ALPHA

UNROLL = 8
TAIL = 16
CHUNK = 4
SLOTS = 4
PIECES = 3
MAG_WHH, MAG_COND, MAG_CPL = 0, 1, 2
AHEAD = 9
TANH_SCALE = 2.0 ** 15


def gru_rk4_kernel(nc, x_in, cond_in, wih_in, whh_in, cpl_in, bih_in, bhh_in, bias_in, out):
    T, _, _ = x_in.shape
    K = 4
    B = 64
    KB = K * B
    M3 = 12
    assert T % UNROLL == 0 and T >= TAIL + 2 * UNROLL and UNROLL % (2 * CHUNK) == 0
    assert M3 == CHUNK * PIECES
    LAST_PIECE = T // CHUNK * M3
    FIRST_PIECES = M3 + PIECES

    ctx = ExitStack()
    with ctx:
        def sb(name, shape, dt=F32):
            return ctx.enter_context(nc.sbuf_tensor(name, shape, dt))

        def bank(name):
            return ctx.enter_context(nc.psum_tensor(name, [P, 512], F32))

        def sem(name):
            return ctx.enter_context(nc.semaphore(name))

        wih_hi = sb("wih_hi", [P, K, 1536], F32R)
        wih_lo = sb("wih_lo", [P, K, 1536], F32R)
        whh_hi = sb("whh_hi", [P, K, 1536], F16)
        whh_lo = sb("whh_lo", [P, K, 1536], F16)
        cpl_hi = sb("cpl_hi", [P, K, 512], F16)
        cpl_lo = sb("cpl_lo", [P, K, 512], F16)
        whh_raw = sb("whh_raw", [P, K * 1536])
        cpl_raw = sb("cpl_raw", [P, K * 512])
        gi = [sb(f"gi{i}", [P, M3, CHUNK, B]) for i in range(2)]
        ring = sb("ring", [P, SLOTS, KB])
        xs_raw = sb("xs_raw", [P, SLOTS, KB])
        xs_hi = [sb(f"xs_hi{i}", [P, CHUNK, K, B], F32R) for i in range(2)]
        xs_lo = [sb(f"xs_lo{i}", [P, CHUNK, K, B], F32R) for i in range(2)]

        bih = sb("bih", [P, M3])
        bhh = sb("bhh", [P, M3])
        gi_bias = sb("gi_bias", [P, M3])
        rk_bias = sb("rk_bias", [P, K])
        whh_mags = sb("whh_mags", [P, K])
        mags = sb("mags", [P, 3])
        allmags = sb("allmags", [P, 3])
        pow2 = sb("pow2", [P, 3])
        scale = sb("scale", [P, 3])
        gh_unscale = sb("gh_unscale", [P, 1])
        rk_unscale = sb("rk_unscale", [P, 4])

        q = sb("q", [P, 4, KB])
        q_raw = sb("q_raw", [P, KB])
        th = sb("th", [P, KB])
        th_hi = sb("th_hi", [P, KB], F16)
        th_lo = sb("th_lo", [P, KB], F16)
        sq = sb("sq", [P, KB])
        cube = sb("cube", [P, KB])
        b_state = sb("b_state", [P, KB])
        b_raw = sb("b_raw", [P, KB])
        b_mid = sb("b_mid", [P, KB])
        y = sb("y", [P, 4, KB])
        y_sum = sb("y_sum", [P, KB])
        drive = sb("drive", [P, KB])
        e = sb("e", [P, KB])
        lin = sb("lin", [P, 3, KB])
        lin_full = sb("lin_full", [P, KB])
        lin_end = sb("lin_end", [P, KB])
        base = sb("base", [P, 4, KB])
        q_sum = sb("q_sum", [P, KB])

        h = sb("h", [P, KB])
        h_hi = sb("h_hi", [P, KB], F16)
        h_lo = sb("h_lo", [P, KB], F16)
        rz_in = sb("rz_in", [P, 2 * KB])
        rz = sb("rz", [P, 2 * KB])
        n_h = sb("n_h", [P, KB])
        n_rh = sb("n_rh", [P, KB])
        n_in = sb("n_in", [P, KB])
        n_gate = sb("n_gate", [P, KB])
        h_minus_n = sb("h_minus_n", [P, KB])
        z_part = sb("z_part", [P, KB])

        ps_rk = bank("ps_rk")
        ps_rz = bank("ps_rz")
        ps_n = bank("ps_n")
        ps_gi = [bank(f"ps_gi{i}") for i in range(PIECES)]
        start_banks = ps_gi + [ps_rk, ps_rz, ps_n]

        wih_loaded = [sem(f"wih_loaded{k}") for k in range(K)]
        whh_loaded = [sem(f"whh_loaded{k}") for k in range(K)]
        cpl_loaded = sem("cpl_loaded")
        cond_loaded = sem("cond_loaded")
        bias_loaded = sem("bias_loaded")
        x_loaded = [sem(f"x_loaded{i}") for i in range(SLOTS)]
        xs_loaded = [sem(f"xs_loaded{i}") for i in range(SLOTS)]
        stored = [sem(f"stored{i}") for i in range(SLOTS)]
        wih_hi_ready = sem("wih_hi_ready")
        wih_lo_ready = sem("wih_lo_ready")
        mags_ready = sem("mags_ready")
        allmags_ready = sem("allmags_ready")
        consts_ready = sem("consts_ready")
        max_steps = sem("max_steps")
        whh_scaling = sem("whh_scaling")
        cpl_scaling = sem("cpl_scaling")
        whh_hi_ready = sem("whh_hi_ready")
        whh_lo_ready = sem("whh_lo_ready")
        cpl_hi_ready = sem("cpl_hi_ready")
        cpl_lo_ready = sem("cpl_lo_ready")
        gi_bias_ready = sem("gi_bias_ready")
        xs_hi_ready = sem("xs_hi_ready")
        xs_lo_ready = sem("xs_lo_ready")
        gi_summed = sem("gi_summed")
        gi_ready = sem("gi_ready")
        rz_summed = sem("rz_summed")
        n_summed = sem("n_summed")
        rz_in_ready = sem("rz_in_ready")
        rz_ready = sem("rz_ready")
        n_h_ready = sem("n_h_ready")
        n_rh_ready = sem("n_rh_ready")
        n_in_ready = sem("n_in_ready")
        n_gate_ready = sem("n_gate_ready")
        h_minus_n_ready = sem("h_minus_n_ready")
        z_part_ready = sem("z_part_ready")
        h_ready = sem("h_ready")
        h_hi_ready = sem("h_hi_ready")
        h_lo_ready = sem("h_lo_ready")
        x1_ready = sem("x1_ready")
        drive_ready = sem("drive_ready")
        rk_summed = sem("rk_summed")
        q_ready = sem("q_ready")
        q_raw_ready = sem("q_raw_ready")
        th_ready = sem("th_ready")
        th_hi_ready = sem("th_hi_ready")
        th_lo_ready = sem("th_lo_ready")
        sq_ready = sem("sq_ready")
        cube_ready = sem("cube_ready")
        y_ready = sem("y_ready")
        b_mid_ready = sem("b_mid_ready")
        b_raw_ready = sem("b_raw_ready")
        b_ready = sem("b_ready")
        e_ready = sem("e_ready")
        lin_ready = sem("lin_ready")
        lin_full_ready = sem("lin_full_ready")
        lin_end0_ready = sem("lin_end0_ready")
        lin_end_ready = sem("lin_end_ready")
        base0_ready = sem("base0_ready")
        base_ready = sem("base_ready")
        base3_ready = sem("base3_ready")
        y12_ready = sem("y12_ready")
        y_part_ready = sem("y_part_ready")
        y_sum_ready = sem("y_sum_ready")
        q_part_ready = sem("q_part_ready")
        q_sum1_ready = sem("q_sum1_ready")
        q_sum_ready = sem("q_sum_ready")
        out_ready = sem("out_ready")

        def wait(eng, s, value):
            if not isinstance(value, int) or value > 0:
                eng.wait_ge(s, value)

        def over_steps(eng, step):
            for j in range(UNROLL):
                step(0, j)
            with eng.Fori(UNROLL, T - TAIL - UNROLL + 1, UNROLL) as t0:
                for j in range(UNROLL):
                    step(t0, j)
            for j in range(TAIL):
                step(T - TAIL, j)

        def before(t0, j, limit):
            return not isinstance(t0, int) or t0 + j < limit

        def rounds(t0, j):
            return t0 * (16 // SLOTS) + 16 * (j // SLOTS + 1)

        def x_at(dram, t0, j):
            if isinstance(t0, int):
                return dram[t0 + j, :, :]
            return dram[bass.ds(t0 + j, 1), :, :].rearrange("t p n -> p (t n)")

        def splits_x(t0, j):
            return before(t0, j + AHEAD, T)

        block = ctx.enter_context(nc.Block())

        @block.sync
        def _(sp):
            for u in range(SLOTS):
                sp.dma_start(ring[:, u, :], x_at(x_in, 0, u)).then_inc(x_loaded[u], 16)
            for k in range(K):
                raw = gi[k // 2][:, :, :, :].rearrange("p m j b -> p (m j b)")
                sp.dma_start(raw[:, k % 2 * 1536:(k % 2 + 1) * 1536], wih_in[:, k, :]).then_inc(wih_loaded[k], 16)
            sp.dma_start(bih[:, :], bih_in).then_inc(bias_loaded, 16)
            sp.dma_start(bhh[:, :], bhh_in).then_inc(bias_loaded, 16)
            sp.dma_start(rk_bias[:, :], bias_in).then_inc(bias_loaded, 16)
            for u in range(SLOTS, 2 * SLOTS):
                sp.dma_start(xs_raw[:, u % SLOTS, :], x_at(x_in, 0, u)).then_inc(xs_loaded[u % SLOTS], 16)
            sp.dma_start(q[:, 0, :], cond_in).then_inc(cond_loaded, 16)
            sp.dma_start(h[:, :], cond_in).then_inc(cond_loaded, 16)
            for k in range(K):
                sp.dma_start(whh_raw[:, k * 1536:(k + 1) * 1536], whh_in[:, k * 1536:(k + 1) * 1536]).then_inc(whh_loaded[k], 16)
            sp.dma_start(cpl_raw[:, :], cpl_in).then_inc(cpl_loaded, 16)

            def refill_xs(t0, u):
                sp.wait_ge(xs_lo_ready, t0 + (u - SLOTS + 1))
                sp.dma_start(xs_raw[:, u % SLOTS, :], x_at(x_in, t0, u)).then_inc(xs_loaded[u % SLOTS], 16)

            for u in range(2 * SLOTS, AHEAD + SLOTS):
                refill_xs(0, u)

            def step(t0, j):
                if before(t0, j + AHEAD + SLOTS, T):
                    refill_xs(t0, j + AHEAD + SLOTS)
                if (not isinstance(t0, int) or t0 + j >= 1) and before(t0, j - 1 + SLOTS, T):
                    slot = (j - 1) % SLOTS
                    sp.wait_ge(stored[slot], rounds(t0, j - 1))
                    sp.dma_start(ring[:, slot, :], x_at(x_in, t0, j - 1 + SLOTS)).then_inc(x_loaded[slot], 16)
                sp.wait_ge(out_ready, t0 + (j + 1))
                sp.dma_start(x_at(out, t0, j), ring[:, j % SLOTS, :]).then_inc(stored[j % SLOTS], 16)
            over_steps(sp, step)
            for s in stored:
                sp.wait_ge(s, 16 * (T // SLOTS))

        @block.tensor
        def _(pe):
            def product(ps, cols, w_hi, w_lo, w_cols, v_hi, v_lo, done, first=0, end=None, before_lo=None):
                count = 3 * cols * K
                for n in range(first, count if end is None else end):
                    part, r = divmod(n, cols * K)
                    m, k = divmod(r, K)
                    if part == 2 and r == 0 and before_lo is not None:
                        before_lo()
                    w = w_lo if part == 0 else w_hi
                    v = v_lo if part == 2 else v_hi
                    mm = nc.tensor.matmul(ps[:, m * B:(m + 1) * B], w[:, k, w_cols + m * P:w_cols + (m + 1) * P],
                                          v[:, k * B:(k + 1) * B], start=(n == 0), stop=(n == count - 1),
                                          skip_group_check=True)
                    if n == count - 1:
                        mm.then_inc(done, 1)

            def coupling(t0, j, s):
                pe.wait_ge(th_hi_ready, t0 * 4 + (4 * j + s + 1))
                product(ps_rk, K, cpl_hi, cpl_lo, 0, th_hi, th_lo, rk_summed,
                        before_lo=lambda: pe.wait_ge(th_lo_ready, t0 * 4 + (4 * j + s + 1)))

            def gates_rz(t0, j, first=0, end=None):
                if first == 0:
                    pe.wait_ge(h_lo_ready, t0 + (j + 1))
                product(ps_rz, 2 * K, whh_hi, whh_lo, 0, h_hi, h_lo, rz_summed, first, end)

            def gates_n(t0, j):
                pe.wait_ge(h_lo_ready, t0 + (j + 1))
                product(ps_n, K, whh_hi, whh_lo, 8 * P, h_hi, h_lo, n_summed)

            def project(t0, first, lo, hi):
                for n in range(lo, hi):
                    i, r = divmod(n, 3 * K)
                    k, part = divmod(r, 3)
                    g = first + i
                    m = g % M3
                    par = g // M3 % 2
                    if r == 0:
                        wait(pe, gi_ready, t0 * 3 + (g - PIECES + 1))
                    if part == 2:
                        w, v = wih_lo, xs_hi[par]
                    else:
                        w, v = wih_hi, (xs_hi, xs_lo)[part][par]
                    last = nc.tensor.matmul(ps_gi[i][:, 0:CHUNK * B].rearrange("p (j b) -> p j b", j=CHUNK),
                                            w[:, k, m * P:(m + 1) * P], v[:, :, k, :],
                                            start=(r == 0), stop=(r == 3 * K - 1))
                    if r == 3 * K - 1:
                        last.then_inc(gi_summed, 1)

            pe.wait_ge(xs_hi_ready, CHUNK)
            pe.wait_ge(xs_lo_ready, CHUNK)
            for k in range(K):
                for part in range(3):
                    if part == 0:
                        pe.wait_ge(wih_hi_ready, k + 1)
                    if part == 2:
                        pe.wait_ge(wih_lo_ready, k + 1)
                    w, v = (wih_lo if part == 2 else wih_hi), (xs_lo[0] if part == 1 else xs_hi[0])
                    for m, ps in enumerate(start_banks):
                        last = nc.tensor.matmul(ps[:, 0:CHUNK * B].rearrange("p (j b) -> p j b", j=CHUNK),
                                                w[:, k, m * P:(m + 1) * P], v[:, :, k, :],
                                                start=(k == 0 and part == 0), stop=(k == K - 1 and part == 2))
                        if k == K - 1 and part == 2:
                            last.then_inc(gi_summed, 1)
            for first in range(len(start_banks), M3, PIECES):
                project(0, first, 0, PIECES * 3 * K)

            pe.wait_ge(h_hi_ready, 1)
            pe.wait_ge(h_lo_ready, 1)
            pe.wait_ge(gi_ready, len(start_banks))
            for part, w, v in ((0, whh_hi, h_hi), (1, whh_hi, h_lo), (2, whh_lo, h_hi)):
                for k in range(K):
                    if part == 0:
                        pe.wait_ge(whh_hi_ready, k + 1)
                    if part == 2:
                        pe.wait_ge(whh_lo_ready, k + 1)
                    for m in range(M3):
                        ps, col = (ps_rz, m) if m < 2 * K else (ps_n, m - 2 * K)
                        last = nc.tensor.matmul(ps[:, col * B:(col + 1) * B], w[:, k, m * P:(m + 1) * P],
                                                v[:, k * B:(k + 1) * B], start=(part == 0 and k == 0 and col == 0),
                                                stop=(part == 2 and k == K - 1), skip_group_check=True)
                        if part == 2 and k == K - 1 and m in (2 * K - 1, M3 - 1):
                            last.then_inc(rz_summed if m < 2 * K else n_summed, 1)
            pe.wait_ge(xs_hi_ready, 2 * CHUNK)
            pe.wait_ge(xs_lo_ready, 2 * CHUNK)
            project(0, M3, 0, PIECES * 3 * K)
            pe.wait_ge(cpl_lo_ready, K)

            def step(t0, j):
                more_cells = before(t0, j + 1, T)
                first = FIRST_PIECES + 3 * j
                more_pieces = not isinstance(t0, int) or t0 * 3 + first < LAST_PIECE
                coupling(t0, j, 0)
                if more_cells:
                    gates_rz(t0, j + 1, 0, 72)
                coupling(t0, j, 1)
                if more_cells:
                    gates_rz(t0, j + 1, 72)
                    gates_n(t0, j + 1)
                coupling(t0, j, 2)
                if more_pieces:
                    pe.wait_ge(xs_hi_ready, t0 + CHUNK * (first // M3 + 1))
                    pe.wait_ge(xs_lo_ready, t0 + CHUNK * (first // M3 + 1))
                    project(t0, first, 0, 18)
                coupling(t0, j, 3)
                if more_pieces:
                    project(t0, first, 18, 36)
            over_steps(pe, step)

        @block.scalar
        def _(act):
            def split_x_hi(t0, u):
                if isinstance(t0, int) and t0 + u < SLOTS:
                    act.wait_ge(x_loaded[u], 16)
                    src = ring
                else:
                    act.wait_ge(xs_loaded[u % SLOTS], rounds(t0, u - SLOTS))
                    src = xs_raw
                nc.scalar.activation(xs_hi[u // CHUNK % 2][:, u % CHUNK, :, :].rearrange("p k b -> p (k b)"),
                                     src[:, u % SLOTS, :], ACT.Copy).then_inc(xs_hi_ready, 1)

            def store_gi(t0, g, ps=None):
                act.wait_ge(gi_summed, t0 * 3 + (g + 1))
                m = g % M3
                nc.scalar.activation(gi[g // M3 % 2][:, m, :, :].rearrange("p j b -> p (j b)"),
                                     (ps or ps_gi[g % PIECES])[:, 0:CHUNK * B], ACT.Identity,
                                     bias=gi_bias[:, m:m + 1], scale=1.0).then_inc(gi_ready, 1)

            def gate_rz(t0, j):
                act.wait_ge(rz_in_ready, t0 + (j + 1))
                nc.scalar.activation(rz[:, :], rz_in[:, :], ACT.Tanh, scale=0.5).then_inc(rz_ready, 1)

            def split_h_hi(t0, u):
                act.wait_ge(h_ready, t0 + (u + 1))
                nc.scalar.activation(h_hi[:, :], h[:, :], ACT.Copy, scale=scale[:, MAG_COND:MAG_COND + 1]).then_inc(h_hi_ready, 1)

            def gate_n(t0, j):
                act.wait_ge(n_in_ready, t0 + (j + 1))
                nc.scalar.activation(n_gate[:, :], n_in[:, :], ACT.Tanh).then_inc(n_gate_ready, 1)

            def tanh(t0, j, s):
                wait(act, q_ready, t0 * 4 + (4 * j + s))
                wait(act, th_lo_ready, t0 * 4 + (4 * j + s))
                nc.scalar.activation(th[:, :], q[:, s, :], ACT.Tanh).then_inc(th_ready, 1)

            def tanh_hi(t0, j, s):
                act.wait_ge(th_ready, t0 * 4 + (4 * j + s + 1))
                nc.scalar.activation(th_hi[:, :], th[:, :], ACT.Copy, scale=TANH_SCALE).then_inc(th_hi_ready, 1)

            def square(t0, j, s):
                wait(act, cube_ready, t0 * 4 + (4 * j + s))
                nc.scalar.activation(sq[:, :], q[:, s, :], ACT.Square,
                                     scale=(STAGE_DT[s] / 3) ** 0.5).then_inc(sq_ready, 1)

            for u in range(CHUNK):
                split_x_hi(0, u)
            for k in range(K):
                act.wait_ge(wih_loaded[k], 16)
                raw = gi[k // 2][:, :, :, :].rearrange("p m j b -> p (m j b)")
                nc.scalar.activation(wih_hi[:, k, :], raw[:, k % 2 * 1536:(k % 2 + 1) * 1536],
                                     ACT.Copy).then_inc(wih_hi_ready, 1)
            for u in range(CHUNK, 2 * CHUNK):
                split_x_hi(0, u)
            act.wait_ge(gi_bias_ready, 2)
            act.wait_ge(wih_lo_ready, K)
            for g in range(M3 - 2):
                store_gi(0, g, start_banks[g] if g < len(start_banks) else None)
            act.wait_ge(whh_scaling, 6)
            for k in range(K):
                nc.scalar.activation(whh_hi[:, k, :], whh_raw[:, k * 1536:(k + 1) * 1536], ACT.Copy,
                                     scale=scale[:, MAG_WHH:MAG_WHH + 1]).then_inc(whh_hi_ready, 1)
            for g in range(M3 - 2, M3):
                store_gi(0, g)
            for u in range(2 * CHUNK, AHEAD):
                split_x_hi(0, u)
            gate_rz(0, 0)
            act.wait_ge(cpl_scaling, 4)
            for k in range(K):
                nc.scalar.activation(cpl_hi[:, k, :], cpl_raw[:, k * 512:(k + 1) * 512], ACT.Copy,
                                     scale=scale[:, MAG_CPL:MAG_CPL + 1]).then_inc(cpl_hi_ready, 1)
            gate_n(0, 0)
            store_gi(0, M3)
            split_h_hi(0, 0)

            def step(t0, j):
                more_cells = before(t0, j + 1, T)
                first = FIRST_PIECES + 3 * j
                more_pieces = not isinstance(t0, int) or t0 * 3 + first < LAST_PIECE
                late = not isinstance(t0, int) or t0 * 3 + first - PIECES < LAST_PIECE
                tanh(t0, j, 0)
                tanh_hi(t0, j, 0)
                square(t0, j, 0)
                if late:
                    store_gi(t0, first - 2)
                tanh(t0, j, 1)
                tanh_hi(t0, j, 1)
                square(t0, j, 1)
                tanh(t0, j, 2)
                tanh_hi(t0, j, 2)
                square(t0, j, 2)
                if splits_x(t0, j):
                    split_x_hi(t0, j + AHEAD)
                if more_cells:
                    gate_rz(t0, j + 1)
                if late:
                    store_gi(t0, first - 1)
                tanh(t0, j, 3)
                if more_cells:
                    gate_n(t0, j + 1)
                tanh_hi(t0, j, 3)
                square(t0, j, 3)
                if more_pieces:
                    store_gi(t0, first)
                if more_cells:
                    split_h_hi(t0, j + 1)
            over_steps(act, step)

        @block.vector
        def _(dve):
            def fma(dst, a, c, b, done, op1=ALU.add):
                nc.vector.scalar_tensor_tensor(out=dst, in0=a, scalar=c, in1=b, op0=ALU.mult, op1=op1).then_inc(done, 1)

            def cell_rz(t0, u):
                dve.wait_ge(rz_summed, t0 + (u + 1))
                dve.wait_ge(gi_ready, t0 * 3 + (M3 * (u // CHUNK) + 2 * K))
                blocks = gi[u // CHUNK % 2][:, 0:8, u % CHUNK, :]
                fma(rz_in[:, :].rearrange("p (m b) -> p m b", b=B), ps_rz[:, :].rearrange("p (m b) -> p m b", b=B),
                    gh_unscale[:, 0:1], blocks, rz_in_ready)

            def cell_n_h(t0, u):
                dve.wait_ge(n_summed, t0 + (u + 1))
                fma(n_h[:, :].rearrange("p (m b) -> p m b", b=B), ps_n[:, 0:KB].rearrange("p (m b) -> p m b", b=B),
                    gh_unscale[:, 0:1], bhh[:, 8:12].unsqueeze(2).broadcast_to([P, K, B]), n_h_ready)

            def cell_n_rh(t0, u):
                dve.wait_ge(rz_ready, t0 + (u + 1))
                dve.wait_ge(n_h_ready, t0 + (u + 1))
                nc.vector.scalar_tensor_tensor(out=n_rh[:, :], in0=rz[:, 0:KB], scalar=1.0, in1=n_h[:, :],
                                               op0=ALU.add, op1=ALU.mult).then_inc(n_rh_ready, 1)

            def cell_n_in(t0, u):
                dve.wait_ge(n_rh_ready, t0 + (u + 1))
                dve.wait_ge(gi_ready, t0 * 3 + M3 * (u // CHUNK + 1))
                fma(n_in[:, :].rearrange("p (m b) -> p m b", b=B), n_rh[:, :].rearrange("p (m b) -> p m b", b=B),
                    0.5, gi[u // CHUNK % 2][:, 8:12, u % CHUNK, :], n_in_ready)

            def cell_z(t0, u):
                dve.wait_ge(h_minus_n_ready, t0 + (u + 1))
                nc.vector.scalar_tensor_tensor(out=z_part[:, :], in0=rz[:, KB:2 * KB], scalar=1.0, in1=h_minus_n[:, :],
                                               op0=ALU.add, op1=ALU.mult).then_inc(z_part_ready, 1)

            def cell_h(t0, u):
                dve.wait_ge(z_part_ready, t0 + (u + 1))
                wait(dve, x1_ready, t0 + u)
                fma(h[:, :], z_part[:, :], 0.5, n_gate[:, :], h_ready)

            def split_h_lo(t0, u):
                dve.wait_ge(h_hi_ready, t0 + (u + 2))
                fma(h_lo[:, :], h[:, :], scale[:, MAG_COND:MAG_COND + 1], h_hi[:, :], h_lo_ready, ALU.subtract)

            for k in range(K):
                dve.wait_ge(wih_hi_ready, k + 1)
                raw = gi[k // 2][:, :, :, :].rearrange("p m j b -> p (m j b)")
                nc.vector.tensor_tensor(wih_lo[:, k, :], raw[:, k % 2 * 1536:(k % 2 + 1) * 1536],
                                        wih_hi[:, k, :].bitcast(F32), ALU.subtract).then_inc(wih_lo_ready, 1)
            dve.wait_ge(bias_loaded, 48)
            nc.vector.tensor_tensor(gi_bias[:, 0:8], bih[:, 0:8], bhh[:, 0:8], ALU.add).then_inc(gi_bias_ready, 1)
            nc.vector.tensor_copy(gi_bias[:, 8:12], bih[:, 8:12]).then_inc(gi_bias_ready, 1)
            nc.vector.tensor_scalar(rk_bias[:, :], rk_bias[:, :], -ALPHA / BETA, None, op0=ALU.add).then_inc(consts_ready, 1)
            dve.wait_ge(cond_loaded, 32)
            nc.vector.tensor_scalar(b_state[:, :], q[:, 0, :], BETA, -ALPHA, op0=ALU.mult, op1=ALU.add).then_inc(consts_ready, 1)

            def largest(dst, src, done):
                nc.vector.tensor_reduce(dst, src, AX.X, ALU.max, apply_absolute_value=True).then_inc(done, 1)

            def powers(lo, hi, done):
                nc.vector.tensor_scalar(pow2[:, lo:hi].bitcast(I32), mags[:, lo:hi].bitcast(I32), 0x7F800000, None,
                                        op0=ALU.bitwise_and).then_inc(done, 1)
                dve.wait_ge(done, 3 if hi - lo > 1 else 2)
                nc.vector.tensor_scalar(pow2[:, lo:hi], pow2[:, lo:hi], 2.0 ** -14, None, op0=ALU.mult).then_inc(done, 1)
                dve.wait_ge(done, 4 if hi - lo > 1 else 3)
                nc.vector.reciprocal(scale[:, lo:hi], pow2[:, lo:hi]).then_inc(done, 1)

            largest(mags[:, MAG_COND:MAG_COND + 1], q[:, 0, :], max_steps)
            for k in range(K):
                dve.wait_ge(whh_loaded[k], 16)
                largest(whh_mags[:, k:k + 1], whh_raw[:, k * 1536:(k + 1) * 1536], max_steps)
            dve.wait_ge(max_steps, 1 + K)
            largest(mags[:, MAG_WHH:MAG_WHH + 1], whh_mags[:, :], mags_ready)
            dve.wait_ge(allmags_ready, 1)
            nc.vector.tensor_scalar(mags[:, MAG_WHH:MAG_WHH + 1], allmags[:, MAG_WHH:MAG_WHH + 1], 2.0 ** -100, None,
                                    op0=ALU.max).then_inc(whh_scaling, 1)
            nc.vector.tensor_scalar(mags[:, MAG_COND:MAG_COND + 1], allmags[:, MAG_COND:MAG_COND + 1], 1.0, None,
                                    op0=ALU.max).then_inc(whh_scaling, 1)
            dve.wait_ge(whh_scaling, 2)
            powers(MAG_WHH, MAG_COND + 1, whh_scaling)
            nc.vector.tensor_tensor(gh_unscale[:, :], pow2[:, MAG_WHH:MAG_WHH + 1], pow2[:, MAG_COND:MAG_COND + 1],
                                    ALU.mult).then_inc(whh_scaling, 1)
            dve.wait_ge(whh_scaling, 6)
            nc.vector.tensor_scalar(h_hi[:, :], h[:, :], scale[:, MAG_COND:MAG_COND + 1], None, op0=ALU.mult).then_inc(h_hi_ready, 1)
            dve.wait_ge(cpl_loaded, 16)
            largest(mags[:, MAG_CPL:MAG_CPL + 1], cpl_raw[:, :], mags_ready)
            split_h_lo(0, -1)
            for k in range(K):
                dve.wait_ge(whh_hi_ready, k + 1)
                fma(whh_lo[:, k, :], whh_raw[:, k * 1536:(k + 1) * 1536], scale[:, MAG_WHH:MAG_WHH + 1], whh_hi[:, k, :],
                    whh_lo_ready, ALU.subtract)
            dve.wait_ge(allmags_ready, 2)
            nc.vector.tensor_scalar(mags[:, MAG_CPL:MAG_CPL + 1], allmags[:, MAG_CPL:MAG_CPL + 1], 2.0 ** -100, None,
                                    op0=ALU.max).then_inc(cpl_scaling, 1)
            dve.wait_ge(cpl_scaling, 1)
            powers(MAG_CPL, MAG_CPL + 1, cpl_scaling)
            for s in range(4):
                nc.vector.tensor_scalar(rk_unscale[:, s:s + 1], pow2[:, MAG_CPL:MAG_CPL + 1], STAGE_DT[s] / TANH_SCALE, None,
                                        op0=ALU.mult).then_inc(cpl_scaling, 1)

            def split_cpl_lo(k):
                dve.wait_ge(cpl_hi_ready, k + 1)
                fma(cpl_lo[:, k, :], cpl_raw[:, k * 512:(k + 1) * 512], scale[:, MAG_CPL:MAG_CPL + 1], cpl_hi[:, k, :],
                    cpl_lo_ready, ALU.subtract)

            def stage_cube(t0, j, s):
                dve.wait_ge(sq_ready, t0 * 4 + (4 * j + s + 1))
                wait(dve, q_ready, t0 * 4 + (4 * j + s))
                if s == 0:
                    wait(dve, base3_ready, t0 + j)
                elif s == 1:
                    dve.wait_ge(base0_ready, t0 + (j + 1))
                else:
                    dve.wait_ge(base_ready, t0 * 2 + (2 * j + s - 1))
                nc.vector.scalar_tensor_tensor(out=cube[:, :], in0=sq[:, :], scalar=-STAGE_DT[s], in1=q[:, s, :],
                                               op0=ALU.add, op1=ALU.mult).then_inc(cube_ready, 1)

            def split_tanh_lo(t0, j, s):
                dve.wait_ge(th_hi_ready, t0 * 4 + (4 * j + s + 1))
                fma(th_lo[:, :], th[:, :], TANH_SCALE, th_hi[:, :], th_lo_ready, ALU.subtract)

            def stage_q(t0, j, s):
                dve.wait_ge(rk_summed, t0 * 4 + (4 * j + s + 1))
                if s < 3:
                    if s == 0:
                        dve.wait_ge(base0_ready, t0 + (j + 1))
                    else:
                        dve.wait_ge(base_ready, t0 * 2 + (2 * j + s))
                    fma(q[:, s + 1, :], ps_rk[:, 0:KB], rk_unscale[:, s:s + 1], base[:, s, :], q_ready)
                else:
                    dve.wait_ge(base3_ready, t0 + (j + 1))
                    fma(q_raw[:, :], ps_rk[:, 0:KB], rk_unscale[:, s:s + 1], base[:, s, :], q_raw_ready)
                    dve.wait_ge(q_raw_ready, t0 + (j + 1))
                    nc.vector.tensor_scalar(q[:, 0, :], q_raw[:, :], -CLAMP, CLAMP, op0=ALU.max, op1=ALU.min).then_inc(q_ready, 1)

            def start_e(t0, j):
                dve.wait_ge(drive_ready, t0 + (j + 1))
                wait(dve, b_ready, t0 + j)
                fma(e[:, :], b_state[:, :], -1.0 / BETA, drive[:, :], e_ready)

            def start_lin0(t0, j):
                dve.wait_ge(e_ready, t0 + (j + 1))
                wait(dve, q_ready, t0 * 4 + 4 * j)
                fma(lin[:, 0, :], e[:, :], HALF, q[:, 0, :], lin_ready)

            def start_lin_full(t0, j):
                dve.wait_ge(e_ready, t0 + (j + 1))
                fma(lin_full[:, :], e[:, :], DT, q[:, 0, :], lin_full_ready)

            def start_lin_end(t0, j):
                dve.wait_ge(e_ready, t0 + (j + 1))
                fma(lin_end[:, :], e[:, :], HALF, q[:, 0, :], lin_end0_ready, ALU.subtract)

            def stage0_base(t0, j):
                dve.wait_ge(lin_ready, t0 * 3 + (3 * j + 1))
                dve.wait_ge(cube_ready, t0 * 4 + (4 * j + 1))
                nc.vector.tensor_tensor(base[:, 0, :], lin[:, 0, :], cube[:, :], ALU.subtract).then_inc(base0_ready, 1)

            def stage_b(t0, j, s):
                dve.wait_ge(y_ready, t0 * 4 + (4 * j + s + 1))
                fma(b_mid[:, :], y[:, s, :], B_DT[s], b_state[:, :], b_mid_ready)

            def stage_lin(t0, j, s):
                dve.wait_ge(y_ready, t0 * 4 + (4 * j + s))
                if s == 1:
                    dve.wait_ge(lin_ready, t0 * 3 + (3 * j + 1))
                    fma(lin[:, 1, :], y[:, 0, :], -HALF * DRIFT, lin[:, 0, :], lin_ready)
                else:
                    dve.wait_ge(lin_full_ready, t0 + (j + 1))
                    fma(lin[:, 2, :], y[:, 1, :], -DT * DRIFT, lin_full[:, :], lin_ready)

            def end_lin(t0, j):
                dve.wait_ge(y_ready, t0 * 4 + (4 * j + 3))
                dve.wait_ge(lin_end0_ready, t0 + (j + 1))
                fma(lin_end[:, :], y[:, 2, :], -DT * DRIFT, lin_end[:, :], lin_end_ready)

            def end_q_part(t0, j):
                dve.wait_ge(q_ready, t0 * 4 + (4 * j + 2))
                fma(q_sum[:, :], q[:, 2, :], 2.0, q[:, 1, :], q_part_ready)

            def end_y(t0, j):
                dve.wait_ge(y12_ready, t0 + (j + 1))
                fma(y_sum[:, :], y_sum[:, :], 2.0, y[:, 0, :], y_part_ready)

            def end_base(t0, j):
                dve.wait_ge(q_sum_ready, t0 + (j + 1))
                dve.wait_ge(cube_ready, t0 * 4 + (4 * j + 4))
                fma(base[:, 3, :], q_sum[:, :], 1.0 / 3, cube[:, :], base3_ready, ALU.subtract)

            def end_b(t0, j):
                dve.wait_ge(y_sum_ready, t0 + (j + 1))
                fma(b_raw[:, :], y_sum[:, :], DRIFT * BETA / 3, b_state[:, :], b_raw_ready)

            def end_b_clip(t0, j):
                dve.wait_ge(b_raw_ready, t0 + (j + 1))
                nc.vector.tensor_scalar(b_state[:, :], b_raw[:, :], B_MIN, B_MAX, op0=ALU.max, op1=ALU.min).then_inc(b_ready, 1)

            cell_rz(0, 0)
            cell_n_h(0, 0)
            cell_n_rh(0, 0)
            cell_n_in(0, 0)
            split_cpl_lo(0)
            split_cpl_lo(1)
            cell_z(0, 0)
            cell_h(0, 0)
            split_cpl_lo(2)
            split_cpl_lo(3)
            dve.wait_ge(cpl_scaling, 8)
            split_h_lo(0, 0)
            start_e(0, 0)
            split_tanh_lo(0, 0, 0)

            def step(t0, j):
                more_cells = before(t0, j + 1, T)
                stage_cube(t0, j, 0)
                start_lin0(t0, j)
                stage0_base(t0, j)

                stage_q(t0, j, 0)
                stage_b(t0, j, 0)
                start_lin_end(t0, j)
                stage_lin(t0, j, 1)
                split_tanh_lo(t0, j, 1)
                stage_cube(t0, j, 1)
                start_lin_full(t0, j)
                stage_lin(t0, j, 2)
                stage_b(t0, j, 1)

                stage_q(t0, j, 1)
                if more_cells:
                    cell_rz(t0, j + 1)
                end_lin(t0, j)
                split_tanh_lo(t0, j, 2)
                stage_cube(t0, j, 2)
                if more_cells:
                    cell_n_h(t0, j + 1)
                end_q_part(t0, j)
                if more_cells:
                    cell_n_rh(t0, j + 1)

                stage_q(t0, j, 2)
                if more_cells:
                    cell_n_in(t0, j + 1)
                end_y(t0, j)
                stage_b(t0, j, 2)
                split_tanh_lo(t0, j, 3)
                stage_cube(t0, j, 3)
                if more_cells:
                    cell_z(t0, j + 1)
                end_base(t0, j)
                if more_cells:
                    cell_h(t0, j + 1)

                stage_q(t0, j, 3)
                end_b(t0, j)
                end_b_clip(t0, j)
                if more_cells:
                    split_h_lo(t0, j + 1)
                    start_e(t0, j + 1)
                    split_tanh_lo(t0, j + 1, 0)
            over_steps(dve, step)

        @block.gpsimd
        def _(pool):
            def tt(dst, a, b, op, done):
                nc.gpsimd.tensor_tensor(dst, a, b, op).then_inc(done, 1)

            def split_x_lo(t0, u):
                pool.wait_ge(xs_hi_ready, t0 + (u + 1))
                half = u // CHUNK % 2
                src = ring if isinstance(t0, int) and t0 + u < SLOTS else xs_raw
                tt(xs_lo[half][:, u % CHUNK, :, :].rearrange("p k b -> p (k b)"), src[:, u % SLOTS, :],
                   xs_hi[half][:, u % CHUNK, :, :].rearrange("p k b -> p (k b)").bitcast(F32), ALU.subtract, xs_lo_ready)

            def cell_d(t0, u):
                pool.wait_ge(n_gate_ready, t0 + (u + 1))
                wait(pool, h_ready, t0 + u)
                tt(h_minus_n[:, :], h[:, :], n_gate[:, :], ALU.subtract, h_minus_n_ready)

            def cell_x1(t0, u):
                pool.wait_ge(x_loaded[u % SLOTS], rounds(t0, u))
                pool.wait_ge(h_ready, t0 + (u + 1))
                tt(ring[:, u % SLOTS, :], ring[:, u % SLOTS, :], h[:, :], ALU.add, x1_ready)

            def cell_drive(t0, u):
                pool.wait_ge(x1_ready, t0 + (u + 1))
                wait(pool, e_ready, t0 + u)
                tt(drive[:, :].rearrange("p (k b) -> p k b", b=B), ring[:, u % SLOTS, :].rearrange("p (k b) -> p k b", b=B),
                   rk_bias[:, :].unsqueeze(2).broadcast_to([P, K, B]), ALU.add, drive_ready)

            for u in range(2 * CHUNK):
                split_x_lo(0, u)
            pool.wait_ge(mags_ready, 1)
            nc.gpsimd.partition_all_reduce(allmags[:, 0:MAG_CPL], mags[:, 0:MAG_CPL], P, RED_MAX).then_inc(allmags_ready, 1)
            pool.wait_ge(mags_ready, 2)
            nc.gpsimd.partition_all_reduce(allmags[:, MAG_CPL:MAG_CPL + 1], mags[:, MAG_CPL:MAG_CPL + 1], P,
                                           RED_MAX).then_inc(allmags_ready, 1)
            for u in range(2 * CHUNK, AHEAD):
                split_x_lo(0, u)
            pool.wait_ge(consts_ready, 2)
            cell_d(0, 0)
            cell_x1(0, 0)
            cell_drive(0, 0)

            def stage_y(t0, j, s):
                wait(pool, q_ready, t0 * 4 + (4 * j + s))
                if s == 0:
                    wait(pool, b_ready, t0 + j)
                    b_s = b_state
                else:
                    pool.wait_ge(b_mid_ready, t0 * 3 + (3 * j + s))
                    b_s = b_mid
                tt(y[:, s, :], q[:, s, :], b_s[:, :], ALU.subtract, y_ready)

            def stage_base(t0, j, s):
                pool.wait_ge(lin_ready, t0 * 3 + (3 * j + s + 1))
                pool.wait_ge(cube_ready, t0 * 4 + (4 * j + s + 1))
                tt(base[:, s, :], lin[:, s, :], cube[:, :], ALU.subtract, base_ready)

            def step(t0, j):
                more_cells = before(t0, j + 1, T)
                if not isinstance(t0, int) or t0 + j >= 1:
                    pool.wait_ge(q_ready, t0 * 4 + 4 * j)
                    tt(ring[:, (j - 1) % SLOTS, :], ring[:, (j - 1) % SLOTS, :], q[:, 0, :], ALU.add, out_ready)
                stage_y(t0, j, 0)
                stage_y(t0, j, 1)
                stage_base(t0, j, 1)
                stage_y(t0, j, 2)
                pool.wait_ge(y_ready, t0 * 4 + (4 * j + 3))
                tt(y_sum[:, :], y[:, 1, :], y[:, 2, :], ALU.add, y12_ready)
                stage_base(t0, j, 2)
                pool.wait_ge(q_part_ready, t0 + (j + 1))
                pool.wait_ge(lin_end_ready, t0 + (j + 1))
                tt(q_sum[:, :], q_sum[:, :], lin_end[:, :], ALU.add, q_sum1_ready)
                pool.wait_ge(q_ready, t0 * 4 + (4 * j + 3))
                pool.wait_ge(q_sum1_ready, t0 + (j + 1))
                tt(q_sum[:, :], q_sum[:, :], q[:, 3, :], ALU.add, q_sum_ready)
                if more_cells:
                    cell_d(t0, j + 1)
                stage_y(t0, j, 3)
                pool.wait_ge(y_ready, t0 * 4 + (4 * j + 4))
                pool.wait_ge(y_part_ready, t0 + (j + 1))
                tt(y_sum[:, :], y_sum[:, :], y[:, 3, :], ALU.add, y_sum_ready)
                if more_cells:
                    cell_x1(t0, j + 1)
                    cell_drive(t0, j + 1)
                if splits_x(t0, j):
                    split_x_lo(t0, j + AHEAD)
            over_steps(pool, step)
            pool.wait_ge(q_ready, 4 * T)
            tt(ring[:, (T - 1) % SLOTS, :], ring[:, (T - 1) % SLOTS, :], q[:, 0, :], ALU.add, out_ready)


def kernel(x, cond_2048, L0_cond_W_ih, L0_cond_W_hh, L0_cond_b_ih, L0_cond_b_hh, L1_cond_coupling, L1_cond_bias):
    import numpy as np
    import concourse.bacc as bacc
    from concourse.bass_utils import run_bass_kernel_spmd

    x, cond, wih, whh, bih, bhh, cpl, bias = (np.asarray(a) for a in (
        x, cond_2048, L0_cond_W_ih, L0_cond_W_hh, L0_cond_b_ih, L0_cond_b_hh, L1_cond_coupling, L1_cond_bias))
    NB, T, D = x.shape
    K = D // 128

    def rows(w):
        return np.ascontiguousarray(w.reshape(K, 128, -1).transpose(1, 0, 2))

    arrays = {
        "x": np.ascontiguousarray(x.reshape(NB, T, K, 128).transpose(1, 3, 2, 0)).reshape(T, 128, K * NB),
        "cond": rows(cond.T).reshape(128, K * NB),
        "wih": rows(wih),
        "whh": rows(whh).reshape(128, K * 3 * D),
        "cpl": rows(cpl.T).reshape(128, K * D),
        "bih": np.ascontiguousarray(bih.reshape(-1, 128).T),
        "bhh": np.ascontiguousarray(bhh.reshape(-1, 128).T),
        "bias": np.ascontiguousarray(bias.reshape(-1, 128).T),
    }
    nc = bacc.Bacc("TRN2", target_bir_lowering=False, num_devices=1)
    args = [nc.dram_tensor(n + "_in", a.shape, mybir.dt.from_np(a.dtype), kind="ExternalInput").ap() for n, a in arrays.items()]
    out = nc.dram_tensor("out", (T, 128, K * NB), F32, kind="ExternalOutput").ap()
    gru_rk4_kernel(nc, *args, out)
    r = run_bass_kernel_spmd(nc, [{n + "_in": a for n, a in arrays.items()}], core_ids=[0])
    got = r.results[0]["out"].reshape(T, 128, K, NB).transpose(3, 0, 2, 1).reshape(NB, T, D)
    return np.ascontiguousarray(got)
```
